# Optimizing a Trainium2 kernel written in Bass

```python
import numpy as np
import jax
import jax.numpy as jnp

def _softmax(x, axis=-1):
    return jax.nn.softmax(x, axis=axis)

def _gelu(x):
    return jax.nn.gelu(x, approximate=True)

def _silu(x):
    return jax.nn.silu(x)

def _sigmoid(x):
    return jax.nn.sigmoid(x)

def _layernorm(x, axis=-1, eps=1e-05):
    m = jnp.mean(x, axis=axis, keepdims=True)
    v = jnp.var(x, axis=axis, keepdims=True)
    return (x - m) / jnp.sqrt(v + eps)

def _scatter_add(tgt, idx, src, axis=0):
    return tgt.at[idx].add(src)

def _segment_sum(src, seg, n):
    return jax.ops.segment_sum(src, seg, n)
kernel_name = 'mk_dlrm_tower_d1_rec_r8_9563c3'

def setup_inputs(seed: int=0):
    np.random.seed(seed)
    _w = jnp.asarray

    def _rec_inputs():
        import jax
        import jax.numpy as jnp
        _tk = jax.random.key(seed)
        dense_ctx = jax.random.normal(jax.random.fold_in(_tk, 190), (2048, 16), jnp.float32)
        ids = jnp.stack([jax.random.randint(jax.random.fold_in(_tk, 200 + f), (2048,), 0, v, jnp.int32) for f, v in enumerate([125000, 125000, 1250, 12500, 12500, 12500, 1000, 125000, 12500, 125000, 1250, 1250, 125000, 1250, 12500, 125000, 1000, 125000, 1250, 125000, 125000, 1000, 1250, 12500, 12500, 1250, 12500, 1250, 1250, 1000, 1250, 125000, 1250, 12500, 1250, 1000, 1250, 1250, 125000])], axis=1)
        tbl_0 = 0.05 * jax.random.normal(jax.random.fold_in(_tk, 500 + 0), (125000, 16), jnp.float32)
        tbl_1 = 0.05 * jax.random.normal(jax.random.fold_in(_tk, 500 + 1), (125000, 16), jnp.float32)
        tbl_2 = 0.05 * jax.random.normal(jax.random.fold_in(_tk, 500 + 2), (1250, 16), jnp.float32)
        tbl_3 = 0.05 * jax.random.normal(jax.random.fold_in(_tk, 500 + 3), (12500, 16), jnp.float32)
        tbl_4 = 0.05 * jax.random.normal(jax.random.fold_in(_tk, 500 + 4), (12500, 16), jnp.float32)
        tbl_5 = 0.05 * jax.random.normal(jax.random.fold_in(_tk, 500 + 5), (12500, 16), jnp.float32)
        tbl_6 = 0.05 * jax.random.normal(jax.random.fold_in(_tk, 500 + 6), (1000, 16), jnp.float32)
        tbl_7 = 0.05 * jax.random.normal(jax.random.fold_in(_tk, 500 + 7), (125000, 16), jnp.float32)
        tbl_8 = 0.05 * jax.random.normal(jax.random.fold_in(_tk, 500 + 8), (12500, 16), jnp.float32)
        tbl_9 = 0.05 * jax.random.normal(jax.random.fold_in(_tk, 500 + 9), (125000, 16), jnp.float32)
        tbl_10 = 0.05 * jax.random.normal(jax.random.fold_in(_tk, 500 + 10), (1250, 16), jnp.float32)
        tbl_11 = 0.05 * jax.random.normal(jax.random.fold_in(_tk, 500 + 11), (1250, 16), jnp.float32)
        tbl_12 = 0.05 * jax.random.normal(jax.random.fold_in(_tk, 500 + 12), (125000, 16), jnp.float32)
        tbl_13 = 0.05 * jax.random.normal(jax.random.fold_in(_tk, 500 + 13), (1250, 16), jnp.float32)
        tbl_14 = 0.05 * jax.random.normal(jax.random.fold_in(_tk, 500 + 14), (12500, 16), jnp.float32)
        tbl_15 = 0.05 * jax.random.normal(jax.random.fold_in(_tk, 500 + 15), (125000, 16), jnp.float32)
        tbl_16 = 0.05 * jax.random.normal(jax.random.fold_in(_tk, 500 + 16), (1000, 16), jnp.float32)
        tbl_17 = 0.05 * jax.random.normal(jax.random.fold_in(_tk, 500 + 17), (125000, 16), jnp.float32)
        tbl_18 = 0.05 * jax.random.normal(jax.random.fold_in(_tk, 500 + 18), (1250, 16), jnp.float32)
        tbl_19 = 0.05 * jax.random.normal(jax.random.fold_in(_tk, 500 + 19), (125000, 16), jnp.float32)
        tbl_20 = 0.05 * jax.random.normal(jax.random.fold_in(_tk, 500 + 20), (125000, 16), jnp.float32)
        tbl_21 = 0.05 * jax.random.normal(jax.random.fold_in(_tk, 500 + 21), (1000, 16), jnp.float32)
        tbl_22 = 0.05 * jax.random.normal(jax.random.fold_in(_tk, 500 + 22), (1250, 16), jnp.float32)
        tbl_23 = 0.05 * jax.random.normal(jax.random.fold_in(_tk, 500 + 23), (12500, 16), jnp.float32)
        tbl_24 = 0.05 * jax.random.normal(jax.random.fold_in(_tk, 500 + 24), (12500, 16), jnp.float32)
        tbl_25 = 0.05 * jax.random.normal(jax.random.fold_in(_tk, 500 + 25), (1250, 16), jnp.float32)
        tbl_26 = 0.05 * jax.random.normal(jax.random.fold_in(_tk, 500 + 26), (12500, 16), jnp.float32)
        tbl_27 = 0.05 * jax.random.normal(jax.random.fold_in(_tk, 500 + 27), (1250, 16), jnp.float32)
        tbl_28 = 0.05 * jax.random.normal(jax.random.fold_in(_tk, 500 + 28), (1250, 16), jnp.float32)
        tbl_29 = 0.05 * jax.random.normal(jax.random.fold_in(_tk, 500 + 29), (1000, 16), jnp.float32)
        tbl_30 = 0.05 * jax.random.normal(jax.random.fold_in(_tk, 500 + 30), (1250, 16), jnp.float32)
        tbl_31 = 0.05 * jax.random.normal(jax.random.fold_in(_tk, 500 + 31), (125000, 16), jnp.float32)
        tbl_32 = 0.05 * jax.random.normal(jax.random.fold_in(_tk, 500 + 32), (1250, 16), jnp.float32)
        tbl_33 = 0.05 * jax.random.normal(jax.random.fold_in(_tk, 500 + 33), (12500, 16), jnp.float32)
        tbl_34 = 0.05 * jax.random.normal(jax.random.fold_in(_tk, 500 + 34), (1250, 16), jnp.float32)
        tbl_35 = 0.05 * jax.random.normal(jax.random.fold_in(_tk, 500 + 35), (1000, 16), jnp.float32)
        tbl_36 = 0.05 * jax.random.normal(jax.random.fold_in(_tk, 500 + 36), (1250, 16), jnp.float32)
        tbl_37 = 0.05 * jax.random.normal(jax.random.fold_in(_tk, 500 + 37), (1250, 16), jnp.float32)
        tbl_38 = 0.05 * jax.random.normal(jax.random.fold_in(_tk, 500 + 38), (125000, 16), jnp.float32)
        _rk = jax.random.fold_in(_tk, 7)
        W_top1 = 0.0606339 * jax.random.normal(jax.random.fold_in(_tk, 801), (272, 512), jnp.float32)
        W_top2 = 0.0441942 * jax.random.normal(jax.random.fold_in(_tk, 802), (512, 256), jnp.float32)
        W_top3 = 0.0625 * jax.random.normal(jax.random.fold_in(_tk, 803), (256, 1), jnp.float32)
        b_top1 = jnp.zeros((512,), jnp.float32)
        b_top2 = jnp.zeros((256,), jnp.float32)
        return (dense_ctx, ids, tbl_0, tbl_1, tbl_2, tbl_3, tbl_4, tbl_5, tbl_6, tbl_7, tbl_8, tbl_9, tbl_10, tbl_11, tbl_12, tbl_13, tbl_14, tbl_15, tbl_16, tbl_17, tbl_18, tbl_19, tbl_20, tbl_21, tbl_22, tbl_23, tbl_24, tbl_25, tbl_26, tbl_27, tbl_28, tbl_29, tbl_30, tbl_31, tbl_32, tbl_33, tbl_34, tbl_35, tbl_36, tbl_37, tbl_38, W_top1, b_top1, W_top2, b_top2, W_top3)
    dense_ctx, ids, tbl_0, tbl_1, tbl_2, tbl_3, tbl_4, tbl_5, tbl_6, tbl_7, tbl_8, tbl_9, tbl_10, tbl_11, tbl_12, tbl_13, tbl_14, tbl_15, tbl_16, tbl_17, tbl_18, tbl_19, tbl_20, tbl_21, tbl_22, tbl_23, tbl_24, tbl_25, tbl_26, tbl_27, tbl_28, tbl_29, tbl_30, tbl_31, tbl_32, tbl_33, tbl_34, tbl_35, tbl_36, tbl_37, tbl_38, W_top1, b_top1, W_top2, b_top2, W_top3 = _rec_inputs()

    def _L0_rec_setup():
        import jax, jax.numpy as jnp
        import numpy as np
        B, F0, D = (256, 39, 16)
        LAYER_SIZES = [128, 128, 128]
        key = jax.random.key(seed)
        ks = jax.random.split(key, 1 + 2 * len(LAYER_SIZES))
        inputs = jax.random.normal(ks[0], (B, F0, D), dtype=jnp.float32)
        out = {'inputs': inputs}
        field_nums = [F0]
        for i, size in enumerate(LAYER_SIZES):
            fk = field_nums[-1]
            fan_in = F0 * fk
            scale = np.sqrt(2.0 / (fan_in + size)).astype(np.float32)
            out[f'w{i}'] = jax.random.normal(ks[1 + 2 * i], (F0, fk, size), dtype=jnp.float32) * scale
            out[f'b{i}'] = jnp.zeros((size,), dtype=jnp.float32)
            field_nums.append(size // 2)
        return out
    _L0_rec_all = _L0_rec_setup()
    _L0_rec_in = {k: v for k, v in _L0_rec_all.items() if k in ('w0', 'w1', 'w2', 'b0', 'b1', 'b2')}
    del _L0_rec_all
    return {'dense_ctx': dense_ctx, 'ids': ids, 'tbl_0': tbl_0, 'tbl_1': tbl_1, 'tbl_2': tbl_2, 'tbl_3': tbl_3, 'tbl_4': tbl_4, 'tbl_5': tbl_5, 'tbl_6': tbl_6, 'tbl_7': tbl_7, 'tbl_8': tbl_8, 'tbl_9': tbl_9, 'tbl_10': tbl_10, 'tbl_11': tbl_11, 'tbl_12': tbl_12, 'tbl_13': tbl_13, 'tbl_14': tbl_14, 'tbl_15': tbl_15, 'tbl_16': tbl_16, 'tbl_17': tbl_17, 'tbl_18': tbl_18, 'tbl_19': tbl_19, 'tbl_20': tbl_20, 'tbl_21': tbl_21, 'tbl_22': tbl_22, 'tbl_23': tbl_23, 'tbl_24': tbl_24, 'tbl_25': tbl_25, 'tbl_26': tbl_26, 'tbl_27': tbl_27, 'tbl_28': tbl_28, 'tbl_29': tbl_29, 'tbl_30': tbl_30, 'tbl_31': tbl_31, 'tbl_32': tbl_32, 'tbl_33': tbl_33, 'tbl_34': tbl_34, 'tbl_35': tbl_35, 'tbl_36': tbl_36, 'tbl_37': tbl_37, 'tbl_38': tbl_38, 'W_top1': W_top1, 'b_top1': b_top1, 'W_top2': W_top2, 'b_top2': b_top2, 'W_top3': W_top3, 'L0_rec_w0': _L0_rec_in['w0'], 'L0_rec_w1': _L0_rec_in['w1'], 'L0_rec_w2': _L0_rec_in['w2'], 'L0_rec_b0': _L0_rec_in['b0'], 'L0_rec_b1': _L0_rec_in['b1'], 'L0_rec_b2': _L0_rec_in['b2']}

def reference(dense_ctx, ids, tbl_0, tbl_1, tbl_2, tbl_3, tbl_4, tbl_5, tbl_6, tbl_7, tbl_8, tbl_9, tbl_10, tbl_11, tbl_12, tbl_13, tbl_14, tbl_15, tbl_16, tbl_17, tbl_18, tbl_19, tbl_20, tbl_21, tbl_22, tbl_23, tbl_24, tbl_25, tbl_26, tbl_27, tbl_28, tbl_29, tbl_30, tbl_31, tbl_32, tbl_33, tbl_34, tbl_35, tbl_36, tbl_37, tbl_38, W_top1, b_top1, W_top2, b_top2, W_top3, L0_rec_w0, L0_rec_w1, L0_rec_w2, L0_rec_b0, L0_rec_b1, L0_rec_b2):
    import jax
    import jax.numpy as jnp

    def _L0_rec_ref(inputs, w0, w1, w2, b0, b1, b2):
        import jax, jax.numpy as jnp
        import numpy as np
        B, F0, D = (256, 39, 16)
        LAYER_SIZES = [128, 128, 128]
        x0 = inputs
        xk = inputs
        params = [(w0, b0), (w1, b1), (w2, b2)]
        n_layers = len(params)
        direct = []
        for idx, (W, b) in enumerate(params):
            z = jnp.einsum('bhd,bkd,hks->bsd', x0, xk, W) + b[None, :, None]
            z = jax.nn.relu(z)
            if idx != n_layers - 1:
                half = z.shape[1] // 2
                xk = z[:, :half, :]
                direct.append(z[:, half:, :])
            else:
                direct.append(z)
        logit = jnp.sum(jnp.concatenate(direct, axis=1), axis=-1)
        return logit
    e = jnp.stack([tbl_0[ids[:, 0]], tbl_1[ids[:, 1]], tbl_2[ids[:, 2]], tbl_3[ids[:, 3]], tbl_4[ids[:, 4]], tbl_5[ids[:, 5]], tbl_6[ids[:, 6]], tbl_7[ids[:, 7]], tbl_8[ids[:, 8]], tbl_9[ids[:, 9]], tbl_10[ids[:, 10]], tbl_11[ids[:, 11]], tbl_12[ids[:, 12]], tbl_13[ids[:, 13]], tbl_14[ids[:, 14]], tbl_15[ids[:, 15]], tbl_16[ids[:, 16]], tbl_17[ids[:, 17]], tbl_18[ids[:, 18]], tbl_19[ids[:, 19]], tbl_20[ids[:, 20]], tbl_21[ids[:, 21]], tbl_22[ids[:, 22]], tbl_23[ids[:, 23]], tbl_24[ids[:, 24]], tbl_25[ids[:, 25]], tbl_26[ids[:, 26]], tbl_27[ids[:, 27]], tbl_28[ids[:, 28]], tbl_29[ids[:, 29]], tbl_30[ids[:, 30]], tbl_31[ids[:, 31]], tbl_32[ids[:, 32]], tbl_33[ids[:, 33]], tbl_34[ids[:, 34]], tbl_35[ids[:, 35]], tbl_36[ids[:, 36]], tbl_37[ids[:, 37]], tbl_38[ids[:, 38]]], axis=1)
    z = _L0_rec_ref(e, L0_rec_w0, L0_rec_w1, L0_rec_w2, L0_rec_b0, L0_rec_b1, L0_rec_b2)
    z = z.reshape(z.shape[0], -1)
    h = jnp.concatenate([z, dense_ctx], axis=1)
    h = jnp.maximum(h @ W_top1 + b_top1, 0.0)
    h = jnp.maximum(h @ W_top2 + b_top2, 0.0)
    y = h @ W_top3
    return y

_drawn_inputs = setup_inputs


def setup_inputs(seed=0):
    import zlib

    import numpy as np

    out = dict(_drawn_inputs(seed))
    spreads = {'b_top1': (0.0, 2.0),
     'b_top2': (0.0, 2.0),
     'L0_rec_b0': (0.0, 0.343),
     'L0_rec_b1': (0.0, 0.538),
     'L0_rec_b2': (0.0, 0.8)}
    factors = {'tbl_0': 8.0,
     'tbl_1': 8.0,
     'tbl_2': 8.0,
     'tbl_3': 8.0,
     'tbl_4': 8.0,
     'tbl_5': 8.0,
     'tbl_6': 8.0,
     'tbl_7': 8.0,
     'tbl_8': 8.0,
     'tbl_9': 8.0,
     'tbl_10': 8.0,
     'tbl_11': 8.0,
     'tbl_12': 8.0,
     'tbl_13': 8.0,
     'tbl_14': 8.0,
     'tbl_15': 8.0,
     'tbl_16': 8.0,
     'tbl_17': 8.0,
     'tbl_18': 8.0,
     'tbl_19': 8.0,
     'tbl_20': 8.0,
     'tbl_21': 8.0,
     'tbl_22': 8.0,
     'tbl_23': 8.0,
     'tbl_24': 8.0,
     'tbl_25': 8.0,
     'tbl_26': 8.0,
     'tbl_27': 8.0,
     'tbl_28': 8.0,
     'tbl_29': 8.0,
     'tbl_30': 8.0,
     'tbl_31': 8.0,
     'tbl_32': 8.0,
     'tbl_33': 8.0,
     'tbl_34': 8.0,
     'tbl_35': 8.0,
     'tbl_36': 8.0,
     'tbl_37': 8.0,
     'tbl_38': 8.0,
     'L0_rec_w0': 8.0,
     'L0_rec_w1': 6.27,
     'L0_rec_w2': 4.759,
     'dense_ctx': 8.0}
    for name, (base, spread) in spreads.items():
        noise = np.random.default_rng([zlib.crc32(name.encode()), seed]).standard_normal(out[name].shape)
        drawn = base * np.exp(spread * noise) if base else spread * noise
        out[name] = jnp.asarray(drawn.astype(out[name].dtype))
    for name, factor in factors.items():
        out[name] = (out[name] * factor).astype(out[name].dtype)
    return out
```

```python
from contextlib import ExitStack

import concourse.bass as bass
from concourse import mybir

F32 = mybir.dt.float32
I32 = mybir.dt.int32
ALU = mybir.AluOpType
ACT = mybir.ActivationFunctionType
AX_X = mybir.AxisListType.X

P = 128
FIELDS = 39
D = 16
S = 128
HALF = S // 2
CH = 512
DC = CH // P
CPB = D // DC
GT = 4
RING = 4

SHIFTS = FIELDS // 2 + 1
JT = 3
T0 = -(-SHIFTS // JT)
ROWS0 = JT * FIELDS
LAST0 = (SHIFTS - JT * (T0 - 1)) * FIELDS
TK = -(-FIELDS // 2)
GK = TK // GT
FRONT = 2
BACK = GK - FRONT
G0 = [range(0, GT), range(GT, T0)]
PER = 2 * GK + len(G0)
TWICE = 2 * FIELDS


def build(nc, dense, ids, tables, w0, w1, w2, b0, b1, b2, wt1, bt1, wt2, bt2, wt3, eye, out):
    B = ids.shape[0]
    BLOCKS = B // P
    N = B * D
    BLOCK_N = P * D
    CHUNKS = BLOCKS * CPB
    H1 = wt1.shape[1]
    H2 = wt2.shape[1]
    M1, M2 = H1 // P, H2 // P
    assert w0.shape == (FIELDS, FIELDS, S) and GK * GT == TK and CPB == 4 and B % CH == 0

    ctx = ExitStack()
    with ctx:
        def sb(name, shape, dt=F32):
            return ctx.enter_context(nc.sbuf_tensor(name, shape, dt))

        def bank(name):
            return ctx.enter_context(nc.psum_tensor(name, [P, CH], F32))

        def sem(name):
            return ctx.enter_context(nc.semaphore(name))

        x0_rows = nc.dram_tensor("x0_rows", (TWICE, N), F32, kind="Internal")

        w0_sb = sb("w0_sb", [P, T0, S])
        w1_sb = sb("w1_sb", [P, TK, S])
        w2_sb = sb("w2_sb", [P, TK, S])
        bias_sb = sb("bias_sb", [P, 3])
        eye_sb = sb("eye_sb", [P, P])
        ids_sb = sb("ids_sb", [P, BLOCKS, FIELDS], I32)
        ids_cur = sb("ids_cur", [P, FIELDS], I32)
        emb = sb("emb", [P, FIELDS, D])
        x0_t = sb("x0_t", [FIELDS, BLOCK_N])
        pair0 = sb("pair0", [ROWS0, T0 + 1, CH])
        xh_front = sb("xh_front", [P, 2, FRONT * GT, CH])
        xh_back = sb("xh_back", [P, BACK * GT, CH])
        prod = sb("prod", [P, RING, GT, CH])
        direct01 = sb("direct01", [P, 2, CH])
        direct2 = sb("direct2", [P, 2, CH])
        part01 = sb("part01", [P, 2, P])
        part2 = sb("part2", [P, 2, P])
        sum01 = sb("sum01", [P, BLOCKS, P])
        sum2 = sb("sum2", [P, BLOCKS + 1, P])
        dense_sb = sb("dense_sb", [P, BLOCKS, dense.shape[1]])
        bt1_sb = sb("bt1_sb", [P, M1])
        bt2_sb = sb("bt2_sb", [P, M2])
        wt3_sb = sb("wt3_sb", [P, M2, 1])
        w0_swapped = prod[0:ROWS0, RING - 1, :, :].rearrange("p g n -> p (g n)")[:, 0:T0 * S] \
            .rearrange("p (t s) -> p t s", t=T0)
        wt1_sb = xh_front[:, 0, 0:2, :]
        wt1d_sb = xh_front[0:D, 0, 2, :]
        wt2_sb = xh_front[:, 0, 3:5, :].rearrange("p a n -> p (a n)").rearrange("p (k m) -> p k m", k=M1)
        dense_t = xh_back[0:D, 0:B // CH, :]
        h1 = xh_back[:, 4:4 + M1, :]
        h2 = xh_back[:, 8:8 + M2, :]
        y_sb = x0_t[0:1, 0:B]

        z = [bank(f"z{layer}") for layer in range(3)]
        xk = [None, bank("xk1"), bank("xk2")]
        turn = [bank("turn0"), bank("turn1")]

        s_ids = sem("ids_loaded")
        s_eye = sem("eye_loaded")
        s_w0 = sem("w0_loaded")
        s_w = sem("w12_loaded")
        s_small = sem("small_loaded")
        s_zeroed = sem("zeroed")
        s_w0sum = sem("w0_summed")
        s_idcur = sem("ids_copied")
        s_blocks = sem("blocks_begun")
        s_gather = sem("gathered")
        s_turn = sem("turned")
        s_turned = sem("turn_evacuated")
        s_x0 = sem("x0_stored")
        s_pair0 = sem("pair0_loaded")
        s_front = [sem("xh_front_loaded0"), sem("xh_front_loaded1")]
        s_back = [sem(f"xh_back_loaded{g}") for g in range(BACK)]
        s_prod = sem("products_made")
        s_free = sem("ring_slots_freed")
        s_act = [sem(f"layer{layer}_activated") for layer in range(3)]
        s_red01 = sem("direct01_reduced")
        s_red2 = sem("direct2_reduced")
        s_sum01 = sem("sum01_ready")
        s_sum2 = sem("sum2_ready")
        s_top = sem("top_weights_loaded")
        s_dt = sem("dense_turned")
        s_dte = sem("dense_t_ready")
        s_h1 = sem("h1_products")
        s_h1a = sem("h1_ready")
        s_h2 = sem("h2_products")
        s_h2a = sem("h2_ready")
        s_y = sem("y_products")
        s_ya = sem("y_ready")
        s_out = sem("out_stored")

        block = ctx.enter_context(nc.Block())

        LEAD = len(G0)
        PER_BLOCK = PER * CPB

        def start_of(t, c):
            return t * PER_BLOCK + (LEAD + c * PER)

        @block.sync
        def _(sp):
            sp.dma_start(ids_sb[:], ids.rearrange("(t p) f -> p t f", p=P)).then_inc(s_ids, 16)
            sp.dma_start(eye_sb[:], eye).then_inc(s_eye, 16)
            sp.wait_ge(s_zeroed, 1)
            for j in range(SHIFTS):
                t, p0 = j // JT, (j % JT) * FIELDS
                for wrap, lo, hi in ((0, 0, FIELDS - j), (1, FIELDS - j, FIELDS)):
                    if lo == hi:
                        continue
                    k0 = lo + j - wrap * FIELDS
                    step = [[(FIELDS + 1) * S, hi - lo], [1, S]]
                    sp.dma_start(w0_sb[p0 + lo:p0 + hi, t, :],
                                 bass.AP(w0.tensor, (lo * FIELDS + k0) * S, step)).then_inc(s_w0, 16)
                    if j:
                        sp.dma_start(w0_swapped[p0 + lo:p0 + hi, t, :],
                                     bass.AP(w0.tensor, (k0 * FIELDS + lo) * S, step)).then_inc(s_w0, 16)

            def store_x0(t):
                sp.wait_ge(s_turned, t * CPB + CPB)
                for copy in range(2):
                    rows = slice(copy * FIELDS, (copy + 1) * FIELDS)
                    sp.dma_start(x0_rows[rows, bass.ds(t * BLOCK_N, BLOCK_N)], x0_t[:]).then_inc(s_x0, 16)

            def load_pair0(n0):
                for jj in range(JT):
                    rows = slice(jj * FIELDS, (jj + 1) * FIELDS)
                    tiles = T0 if jj * FIELDS < LAST0 else T0 - 1
                    sp.dma_start(pair0[rows, 0:tiles, :],
                                 bass.AP(x0_rows, n0 + jj * N, [[N, FIELDS], [JT * N, tiles], [1, CH]])
                                 ).then_inc(s_pair0, 16)
                    sp.dma_start(pair0[rows, T0, :],
                                 bass.AP(x0_rows, n0, [[N, FIELDS], [1, CH]])).then_inc(s_pair0, 16)

            def load_xh(dst, tile, n0, done):
                for odd in range(2):
                    tiles = min(dst.shape[1], (FIELDS - odd + 1) // 2 - tile)
                    sp.dma_start(dst[odd * HALF:(odd + 1) * HALF, 0:tiles, :],
                                 bass.AP(x0_rows, n0 + (2 * tile + odd) * N, [[0, HALF], [2 * N, tiles], [1, CH]])
                                 ).then_inc(done, 16)

            def load_back(g, n0):
                load_xh(xh_back[:, g * GT:(g + 1) * GT, :], (FRONT + g) * GT, n0, s_back[g])

            store_x0(0)
            sp.wait_ge(s_x0, 32)
            sp.wait_ge(s_zeroed, 4)
            load_pair0(0)
            load_xh(xh_front[:, 0], 0, 0, s_front[0])
            for g in range(BACK):
                load_back(g, 0)
            sp.dma_start(w1_sb[:, 0:TK - 1, :], w1.rearrange("h k s -> (h k) s")[0:(TK - 1) * P, :]
                         .rearrange("(t p) s -> p t s", p=P)).then_inc(s_w, 16)
            sp.dma_start(w1_sb[0:HALF, TK - 1, :], w1[FIELDS - 1]).then_inc(s_w, 16)
            sp.dma_start(w2_sb[:, 0:TK - 1, :], w2.rearrange("h k s -> (h k) s")[0:(TK - 1) * P, :]
                         .rearrange("(t p) s -> p t s", p=P)).then_inc(s_w, 16)
            sp.dma_start(w2_sb[0:HALF, TK - 1, :], w2[FIELDS - 1]).then_inc(s_w, 16)

            def step(t, c):
                at = start_of(t, c)
                n0 = t * BLOCK_N + (c + 1) * CH
                if c == 2:
                    store_x0(t + 1)
                if c == CPB - 1:
                    sp.wait_ge(s_x0, t * 32 + 64)
                sp.wait_ge(s_prod, at)
                load_pair0(n0)
                load_xh(xh_front[:, (c + 1) % 2], 0, n0, s_front[(c + 1) % 2])
                for g in range(BACK):
                    sp.wait_ge(s_prod, at + GK + LEAD + FRONT + g + 1)
                    load_back(g, n0)

            with sp.Fori(0, BLOCKS - 1) as t:
                for c in range(CPB):
                    step(t, c)
            for c in range(CPB - 1):
                at = start_of(BLOCKS - 1, c)
                n0 = (BLOCKS - 1) * BLOCK_N + (c + 1) * CH
                sp.wait_ge(s_prod, at)
                load_pair0(n0)
                load_xh(xh_front[:, (c + 1) % 2], 0, n0, s_front[(c + 1) % 2])
                for g in range(BACK):
                    sp.wait_ge(s_prod, at + GK + LEAD + FRONT + g + 1)
                    load_back(g, n0)
            sp.dma_start(wt1_sb, wt1[0:2 * P, :].rearrange("(k p) m -> p k m", p=P)).then_inc(s_top, 16)
            sp.dma_start(wt1d_sb, wt1[2 * P:2 * P + D, :]).then_inc(s_top, 16)
            sp.dma_start(wt2_sb, wt2.rearrange("(k p) m -> p k m", p=P)).then_inc(s_top, 16)
            sp.wait_ge(s_ya, B // CH)
            sp.dma_start(out.rearrange("b o -> o b"), y_sb).then_inc(s_out, 16)
            sp.wait_ge(s_out, 16)

        @block.gpsimd
        def _(pool):
            def gather(t):
                pool.tensor_copy(ids_cur[:], ids_sb[:, bass.ds(t, 1), :]).then_inc(s_idcur, 1)
                pool.wait_ge(s_idcur, t + 1)
                pool.sem_inc(s_blocks, 1)
                for f in range(FIELDS):
                    pool.indirect_dma_start(emb[:, f, :], None, tables[f],
                                            bass.IndirectOffsetOnAxis(ap=ids_cur[:, f:f + 1], axis=0)
                                            ).then_inc(s_gather, 16)

            pool.wait_ge(s_ids, 16)
            gather(0)
            with pool.Fori(1, BLOCKS) as t:
                pool.wait_ge(s_gather, t * (16 * FIELDS))
                pool.wait_ge(s_turn, t * CPB)
                gather(t)

        @block.scalar
        def _(act):
            act.sem_inc(s_act[1], 1)
            act.sem_inc(s_act[2], 1)
            for n, b in enumerate((b0, b1, b2)):
                act.dma_start(bias_sb[:, n:n + 1], b.rearrange("(s o) -> s o", o=1)).then_inc(s_small, 16)
            act.dma_start(bt1_sb[:], bt1.rearrange("(m p) -> p m", p=P), allow_slow_non_contiguous=True).then_inc(s_small, 16)
            act.dma_start(bt2_sb[:], bt2.rearrange("(m p) -> p m", p=P), allow_slow_non_contiguous=True).then_inc(s_small, 16)
            act.dma_start(wt3_sb[:], wt3.rearrange("(k p) o -> p k o", p=P), allow_slow_non_contiguous=True).then_inc(s_small, 16)
            act.dma_start(dense_sb[:], dense.rearrange("(t p) c -> p t c", p=P)).then_inc(s_small, 16)

            def evacuate_turn(t, r):
                act.wait_ge(s_turn, t * CPB + (r + 1))
                act.activation(x0_t[:, r * CH:(r + 1) * CH], turn[r % 2][0:FIELDS, :], ACT.Copy).then_inc(s_turned, 1)

            def relu(dst, layer, lo, hi):
                return act.activation(dst, z[layer][lo:hi, :], ACT.Relu, bias=bias_sb[lo:hi, layer:layer + 1])

            def activate0(slot):
                relu(xk[1][0:HALF, :], 0, 0, HALF)
                relu(xk[1][HALF:S, :], 0, 0, HALF)
                relu(direct01[0:HALF, slot, :], 0, HALF, S).then_inc(s_act[0], 1)

            for r in range(CPB):
                evacuate_turn(0, r)
            act.wait_ge(s_small, 7 * 16)
            act.wait_ge(s_zeroed, 4)
            act.wait_ge(s_free, RING + LEAD)
            activate0(0)

            def step(t, c, last=False):
                at = start_of(t, c)
                done1 = at + GK
                done0 = done1 if last else done1 + LEAD
                act.wait_ge(s_free, done1 + RING)
                act.wait_ge(s_prod, at)
                relu(xk[2][0:HALF, :], 1, 0, HALF)
                relu(xk[2][HALF:S, :], 1, 0, HALF)
                relu(direct01[HALF:S, c % 2, :], 1, HALF, S).then_inc(s_act[1], 1)
                if c == 1 and not last:
                    if not isinstance(t, int) or t < BLOCKS - 1:
                        act.wait_ge(s_x0, t * 32 + 32)
                        evacuate_turn(t + 1, 0)
                        evacuate_turn(t + 1, 1)
                if not last:
                    act.wait_ge(s_free, done0 + RING)
                    act.wait_ge(s_prod, done1)
                    if c % 2:
                        act.wait_ge(s_red01, t * 2 + (c + 1) // 2)
                    activate0((c + 1) % 2)
                act.wait_ge(s_free, done0 + GK + RING)
                if c % 2 == 0:
                    act.wait_ge(s_red2, t * 2 + c // 2 + 1)
                relu(direct2[:, c % 2, :], 2, 0, S).then_inc(s_act[2], 1)
                if c == 1 and (not isinstance(t, int) or t < BLOCKS - 1):
                    evacuate_turn(t + 1, 2)
                    evacuate_turn(t + 1, 3)

            with act.Fori(0, BLOCKS - 1) as t:
                for c in range(CPB):
                    step(t, c)
            for c in range(CPB):
                step(BLOCKS - 1, c, last=c == CPB - 1)

            for r in range(B // CH):
                act.wait_ge(s_dt, r + 1)
                act.activation(dense_t[:, r, :], turn[r % 2][0:D, :], ACT.Copy).then_inc(s_dte, 1)
            for q in range(B // CH):
                for m in range(M1):
                    act.wait_ge(s_h1, q * M1 + m + 1)
                    if q:
                        act.wait_ge(s_h2, q * M2)
                    act.activation(h1[:, m, :], z[m % 2][:], ACT.Relu, bias=bt1_sb[:, m:m + 1]).then_inc(s_h1a, 1)
                for m in range(M2):
                    act.wait_ge(s_h2, q * M2 + m + 1)
                    if q:
                        act.wait_ge(s_y, q)
                    act.activation(h2[:, m, :], xk[1 + m][:], ACT.Relu, bias=bt2_sb[:, m:m + 1]).then_inc(s_h2a, 1)
                act.wait_ge(s_y, q + 1)
                act.activation(y_sb[:, q * CH:(q + 1) * CH], z[2][0:1, :], ACT.Copy).then_inc(s_ya, 1)

        @block.vector
        def _(dve):
            dve.memset(w0_swapped, 0.0).then_inc(s_zeroed, 1)
            dve.memset(pair0[:, T0 - 1, :], 0.0).then_inc(s_zeroed, 1)
            dve.memset(xh_back[HALF:S, BACK * GT - 1, :], 0.0).then_inc(s_zeroed, 1)
            dve.memset(direct2[:], 0.0)
            dve.memset(part2[:], 0.0).then_inc(s_zeroed, 1)
            dve.wait_ge(s_w0, 16 * (4 * (SHIFTS - 1) + 1))
            dve.tensor_tensor(w0_sb[0:ROWS0, 0:T0 - 1, :], w0_sb[0:ROWS0, 0:T0 - 1, :],
                              w0_swapped[:, 0:T0 - 1, :], ALU.add)
            dve.tensor_tensor(w0_sb[0:LAST0, T0 - 1, :], w0_sb[0:LAST0, T0 - 1, :],
                              w0_swapped[0:LAST0, T0 - 1, :], ALU.add).then_inc(s_w0sum, 1)
            dve.wait_ge(s_w0sum, 1)
            dve.sem_inc(s_free, RING)

            def multiply(number, rel, xh, other, rows):
                tiles = xh.shape[1]
                dve.wait_ge(s_free, number + 1)
                dve.tensor_tensor(prod[0:rows, rel % RING, 0:tiles, :], xh,
                                  other.unsqueeze(1).broadcast_to([rows, tiles, CH]),
                                  ALU.mult).then_inc(s_prod, 1)

            def layer0(number, rel, chunk):
                dve.wait_ge(s_pair0, chunk * (16 * 2 * JT) + 16 * 2 * JT)
                for n, tiles in enumerate(G0):
                    multiply(number + n, rel + n, pair0[:, tiles.start:tiles.stop, :], pair0[:, T0, :], ROWS0)

            def layer12(number, rel, c, src):
                for g in range(GK):
                    if g < FRONT:
                        tiles = xh_front[:, c % 2, g * GT:(g + 1) * GT, :]
                    else:
                        tiles = xh_back[:, (g - FRONT) * GT:(g - FRONT + 1) * GT, :]
                    multiply(number + g, rel + g, tiles, src[:], P)

            def reduce(dst, src, done):
                dve.tensor_reduce(dst, src[:].rearrange("p s (d b) -> p b (s d)", b=P), AX_X, ALU.add).then_inc(done, 1)

            layer0(0, 0, 0)

            def step(t, c, last=False):
                at = start_of(t, c)
                rel = LEAD + c * PER
                chunk = t * CPB + c
                dve.wait_ge(s_act[0], chunk + 1)
                dve.wait_ge(s_front[c % 2], t * (32 * CPB // 2) + (c // 2 + 1) * 32)
                for g in range(GK):
                    if g >= FRONT:
                        dve.wait_ge(s_back[g - FRONT], chunk * 32 + 32)
                    tiles = (xh_front[:, c % 2, g * GT:(g + 1) * GT, :] if g < FRONT
                             else xh_back[:, (g - FRONT) * GT:(g - FRONT + 1) * GT, :])
                    multiply(at + g, rel + g, tiles, xk[1][:], P)
                if c == 0:
                    dve.wait_ge(s_act[2], chunk + 1)
                    reduce(part2[:, 1, :], direct2, s_red2)
                    dve.wait_ge(s_red2, t * 2 + 1)
                    dve.tensor_tensor(sum2[:, bass.ds(t, 1), :], part2[:, 0:1, :], part2[:, 1:2, :],
                                      ALU.add).then_inc(s_sum2, 1)
                if c == 2:
                    dve.wait_ge(s_act[2], chunk + 1)
                    reduce(part2[:, 0, :], direct2, s_red2)
                n = GK
                if not last:
                    layer0(at + n, rel + n, chunk + 1)
                    n += LEAD
                dve.wait_ge(s_act[1], chunk + 2)
                if c % 2:
                    reduce(part01[:, c // 2, :], direct01, s_red01)
                layer12(at + n, rel + n, c, xk[2])
                if c == CPB - 1:
                    dve.wait_ge(s_red01, t * 2 + 2)
                    dve.tensor_tensor(sum01[:, bass.ds(t, 1), :], part01[:, 0:1, :], part01[:, 1:2, :],
                                      ALU.add).then_inc(s_sum01, 1)

            with dve.Fori(0, BLOCKS - 1) as t:
                for c in range(CPB):
                    step(t, c)
            for c in range(CPB):
                step(BLOCKS - 1, c, last=c == CPB - 1)
            dve.wait_ge(s_act[2], CHUNKS + 1)
            reduce(part2[:, 1, :], direct2, s_red2)
            dve.wait_ge(s_red2, 2 * BLOCKS + 1)
            dve.tensor_tensor(sum2[:, BLOCKS, :], part2[:, 0, :], part2[:, 1, :], ALU.add).then_inc(s_sum2, 1)

        @block.tensor
        def _(pe):
            def turn_round(r):
                for q in range(DC):
                    mm = pe.transpose(turn[r % 2][0:FIELDS, q * P:(q + 1) * P], emb[:, :, r * DC + q], eye_sb[:])
                mm.then_inc(s_turn, 1)

            def sum_group(number, rel, layer, weights, tiles, first, last, tail):
                pe.wait_ge(s_prod, number + 1)
                rows = ROWS0 if layer == 0 else P
                for n, tile in enumerate(tiles):
                    k = tail if last and n == len(tiles) - 1 else rows
                    mm = pe.matmul(z[layer][:], weights[0:k, tile, :], prod[0:k, rel % RING, n, :],
                                   start=first and n == 0, stop=last and n == len(tiles) - 1)
                mm.then_inc(s_free, 1)

            def layer0(number, rel):
                for n, tiles in enumerate(G0):
                    sum_group(number + n, rel + n, 0, w0_sb, tiles, n == 0, n == LEAD - 1, LAST0)

            def layer12(number, rel, layer, weights):
                for g in range(GK):
                    sum_group(number + g, rel + g, layer, weights, range(g * GT, (g + 1) * GT),
                              g == 0, g == GK - 1, HALF)

            pe.wait_ge(s_eye, 16)
            pe.wait_ge(s_gather, 16 * FIELDS)
            for r in range(CPB):
                if r >= 2:
                    pe.wait_ge(s_turned, r - 1)
                turn_round(r)
            pe.wait_ge(s_w0sum, 1)
            layer0(0, 0)
            pe.wait_ge(s_w, 16 * 4)

            def step(t, c, last=False):
                at = start_of(t, c)
                rel = LEAD + c * PER
                chunk = t * CPB + c
                turns = c == 1 and (not isinstance(t, int) or t < BLOCKS - 1)
                if turns:
                    pe.wait_ge(s_gather, t * (16 * FIELDS) + 2 * 16 * FIELDS)
                    pe.wait_ge(s_turned, t * CPB + CPB)
                pe.wait_ge(s_act[1], chunk + 1)
                layer12(at, rel, 1, w1_sb)
                if turns:
                    turn_round(0)
                    turn_round(1)
                n = GK
                if not last:
                    pe.wait_ge(s_act[0], chunk + 1)
                    layer0(at + n, rel + n)
                    n += LEAD
                if turns:
                    pe.wait_ge(s_turned, t * CPB + (CPB + 2))
                pe.wait_ge(s_act[2], chunk + 1)
                layer12(at + n, rel + n, 2, w2_sb)
                if turns:
                    turn_round(2)
                    turn_round(3)

            with pe.Fori(0, BLOCKS - 1) as t:
                for c in range(CPB):
                    step(t, c)
            for c in range(CPB):
                step(BLOCKS - 1, c, last=c == CPB - 1)

            pe.wait_ge(s_small, 7 * 16)
            for r in range(B // CH):
                if r >= 2:
                    pe.wait_ge(s_dte, r - 1)
                for q in range(DC):
                    mm = pe.transpose(turn[r % 2][0:D, q * P:(q + 1) * P], dense_sb[:, r * DC + q, :], eye_sb[:])
                mm.then_inc(s_dt, 1)
            pe.wait_ge(s_top, 3 * 16)
            pe.wait_ge(s_sum01, BLOCKS)
            pe.wait_ge(s_sum2, BLOCKS + 1)
            pe.wait_ge(s_act[2], CHUNKS + 1)
            for q in range(B // CH):
                blocks = slice(q * DC, (q + 1) * DC)
                cin2 = slice(q * DC + 1, (q + 1) * DC + 1)
                pe.wait_ge(s_dte, q + 1)
                for m in range(M1):
                    if q * M1 + m >= 2:
                        pe.wait_ge(s_h1a, q * M1 + m - 1)
                    cols = slice(m * P, (m + 1) * P)
                    pe.matmul(z[m % 2][:], wt1_sb[:, 0, cols],
                              sum01[:, blocks, :].rearrange("p t b -> p (t b)"), start=True, stop=False)
                    pe.matmul(z[m % 2][:], wt1_sb[:, 1, cols],
                              sum2[:, cin2, :].rearrange("p t b -> p (t b)"), start=False, stop=False)
                    pe.matmul(z[m % 2][:], wt1d_sb[:, cols], dense_t[:, q, :],
                              start=False, stop=True).then_inc(s_h1, 1)
                for m in range(M2):
                    if q:
                        pe.wait_ge(s_h2a, q * M2 - M2 + m + 1)
                    for k in range(M1):
                        pe.wait_ge(s_h1a, q * M1 + k + 1)
                        mm = pe.matmul(xk[1 + m][:], wt2_sb[:, k, m * P:(m + 1) * P], h1[:, k, :],
                                       start=k == 0, stop=k == M1 - 1)
                    mm.then_inc(s_h2, 1)
                if q:
                    pe.wait_ge(s_ya, q)
                pe.wait_ge(s_h2a, (q + 1) * M2)
                for k in range(M2):
                    mm = pe.matmul(z[2][0:1, :], wt3_sb[:, k, :], h2[:, k, :], start=k == 0, stop=k == M2 - 1)
                mm.then_inc(s_y, 1)


_TABLES = [f"tbl_{f}" for f in range(FIELDS)]
_INS = ["dense_ctx", "ids", *_TABLES, "L0_rec_w0", "L0_rec_w1", "L0_rec_w2", "L0_rec_b0", "L0_rec_b1",
        "L0_rec_b2", "W_top1", "b_top1", "W_top2", "b_top2", "W_top3"]


def kernel(**inputs):
    import numpy as np
    import concourse.bacc as bacc
    from concourse.bass_utils import run_bass_kernel_spmd

    nc = bacc.Bacc("TRN2", target_bir_lowering=False, num_devices=1)
    arrays, aps = {}, {}
    for name in _INS:
        a = np.ascontiguousarray(inputs[name])
        arrays[f"in_{name}_dram"] = a
        aps[name] = nc.dram_tensor(f"in_{name}_dram", a.shape, mybir.dt.from_np(a.dtype), kind="ExternalInput").ap()
    arrays["in_eye_dram"] = np.eye(P, dtype=np.float32)
    eye = nc.dram_tensor("in_eye_dram", (P, P), F32, kind="ExternalInput").ap()
    out = nc.dram_tensor("out_0_dram", (inputs["ids"].shape[0], 1), F32, kind="ExternalOutput").ap()
    rest = [aps[name] for name in _INS[2 + FIELDS:]]
    build(nc, aps["dense_ctx"], aps["ids"], [aps[name] for name in _TABLES], *rest, eye, out)
    r = run_bass_kernel_spmd(nc, [arrays], core_ids=[0])
    return r.results[0]["out_0_dram"]
```

```python
from contextlib import ExitStack

import concourse.bass as bass
from concourse import mybir

F32 = mybir.dt.float32
F32R = mybir.dt.float32r
I32 = mybir.dt.int32
ALU = mybir.AluOpType
ACT = mybir.ActivationFunctionType
AX_X = mybir.AxisListType.X

P = 128
FIELDS = 39
D = 16
S = 128
HALF = S // 2
CH = 512
DC = CH // P
CPB = D // DC
GT = 4
RING = 4

SHIFTS = FIELDS // 2 + 1
JT = 3
T0 = -(-SHIFTS // JT)
ROWS0 = JT * FIELDS
LAST0 = (SHIFTS - JT * (T0 - 1)) * FIELDS
TK = -(-FIELDS // 2)
GK = TK // GT
FRONT = 1
BACK = GK - FRONT
G0 = [range(0, GT), range(GT, T0)]
PER = 2 * GK + len(G0)
K0 = GK
K2 = GK + len(G0)
SPLIT = {0: "pool", 2: "pool", 3: "dve", 5: "pool", 9: "dve", 11: "dve"}
LOOKUPS = (0, 4, 9)
HL = 2
TWICE = 2 * FIELDS


def group_tiles(k):
    if k < K0:
        return 1, range(k * GT, (k + 1) * GT)
    if k < K2:
        return 0, G0[k - K0]
    return 2, range((k - K2) * GT, (k - K2 + 1) * GT)


SPLIT_TILES = [(group_tiles(k)[0], n) for k in range(PER) if k in SPLIT for n in group_tiles(k)[1]]
PLAIN_TILES = [(group_tiles(k)[0], n) for k in range(PER) if k not in SPLIT for n in group_tiles(k)[1]]
SPLIT_ORDER = sorted(SPLIT)


def tile_rows(layer, tile):
    if layer == 0:
        return LAST0 if tile == T0 - 1 else ROWS0
    return HALF if tile == TK - 1 else P


def build(nc, dense, ids, tables, w0, w1, w2, b0, b1, b2, wt1, bt1, wt2, bt2, wt3, eye, out):
    B = ids.shape[0]
    BLOCKS = B // P
    N = B * D
    BLOCK_N = P * D
    CHUNKS = BLOCKS * CPB
    H1 = wt1.shape[1]
    H2 = wt2.shape[1]
    M1, M2 = H1 // P, H2 // P
    assert w0.shape == (FIELDS, FIELDS, S) and GK * GT == TK and CPB == 4 and B % CH == 0

    ctx = ExitStack()
    with ctx:
        def sb(name, shape, dt=F32):
            return ctx.enter_context(nc.sbuf_tensor(name, shape, dt))

        def bank(name):
            return ctx.enter_context(nc.psum_tensor(name, [P, CH], F32))

        def sem(name):
            return ctx.enter_context(nc.semaphore(name))

        x0_rows = nc.dram_tensor("x0_rows", (TWICE, N), F32, kind="Internal")

        w_plain = sb("w_plain", [P, len(PLAIN_TILES), S])
        w_high = sb("w_high", [P, len(SPLIT_TILES), S], F32R)
        w_low = sb("w_low", [P, len(SPLIT_TILES), S], F32R)
        bias_sb = sb("bias_sb", [P, 3])
        eye_sb = sb("eye_sb", [P, P])
        ids_sb = sb("ids_sb", [P, BLOCKS, FIELDS], I32)
        ids_cur = sb("ids_cur", [P, FIELDS], I32)
        emb = sb("emb", [P, FIELDS, D])
        x0_t = sb("x0_t", [FIELDS, BLOCK_N])
        pair0 = sb("pair0", [P, T0 + 1, CH])
        xh_front = sb("xh_front", [P, 2, FRONT * GT, CH])
        xh_back = sb("xh_back", [P, BACK * GT, CH])
        prod = sb("prod", [P, RING, GT, CH])
        high = sb("high", [P, HL, GT, CH], F32R)
        low = sb("low", [P, HL, GT, CH], F32R)
        direct01 = sb("direct01", [P, 2, CH])
        direct2 = sb("direct2", [P, 2, CH])
        part01 = sb("part01", [P, 2, P])
        part2 = sb("part2", [P, 2, P])
        sum01 = sb("sum01", [P, BLOCKS, P])
        sum2 = sb("sum2", [P, BLOCKS + 1, P])
        dense_sb = sb("dense_sb", [P, BLOCKS, dense.shape[1]])
        bt1_sb = sb("bt1_sb", [P, M1])
        bt2_sb = sb("bt2_sb", [P, M2])
        wt3_sb = sb("wt3_sb", [P, M2, 1])
        stage = prod[:].rearrange("p r g n -> p (r g n)").rearrange("p (t s) -> p t s", s=S)
        w_stage = stage[:, 0:len(SPLIT_TILES), :]
        w0_swapped = stage[:, len(SPLIT_TILES):len(SPLIT_TILES) + T0, :]
        wt1_sb = xh_front[:, 0, 0:2, :]
        wt1d_sb = xh_front[0:D, 0, 2, :]
        wt2_sb = pair0[:, 0:2, :].rearrange("p a n -> p (a n)").rearrange("p (k m) -> p k m", k=M1)
        dense_t = xh_back[0:D, 0:B // CH, :]
        h1 = xh_back[:, 4:4 + M1, :]
        h2 = xh_back[:, 8:8 + M2, :]
        y_sb = x0_t[0:1, 0:B]

        z = [bank(f"z{layer}") for layer in range(3)]
        xk = [None, bank("xk1"), bank("xk2")]
        turn = [bank("turn0"), bank("turn1")]

        s_ids = sem("ids_loaded")
        s_eye = sem("eye_loaded")
        s_w0 = sem("w0_loaded")
        s_w = sem("w12_loaded")
        s_small = sem("small_loaded")
        s_zeroed = sem("zeroed")
        s_w0sum = sem("w0_summed")
        s_whigh = sem("w_high_ready")
        s_wlow = sem("w_low_ready")
        s_idcur = sem("ids_copied")
        s_blocks = sem("blocks_begun")
        s_gather = sem("gathered")
        s_turn = sem("turned")
        s_turned = sem("turn_evacuated")
        s_x0 = sem("x0_stored")
        s_pair0 = sem("pair0_loaded")
        s_front = [sem("xh_front_loaded0"), sem("xh_front_loaded1")]
        s_back = [sem(f"xh_back_loaded{g}") for g in range(BACK)]
        s_xk = [None, sem("xk1_ready"), sem("xk2_ready")]
        s_prod = sem("products_made")
        s_high = sem("highs_made")
        s_low = {"dve": sem("lows_made_dve"), "pool": sem("lows_made_pool")}
        s_summed = sem("groups_summed")
        s_act = [sem(f"layer{layer}_activated") for layer in range(3)]
        s_red01 = sem("direct01_reduced")
        s_red2 = sem("direct2_reduced")
        s_sum01 = sem("sum01_ready")
        s_sum2 = sem("sum2_ready")
        s_top = sem("top_weights_loaded")
        s_dt = sem("dense_turned")
        s_dte = sem("dense_t_ready")
        s_h1 = sem("h1_products")
        s_h1a = sem("h1_ready")
        s_h2 = sem("h2_products")
        s_h2a = sem("h2_ready")
        s_y = sem("y_products")
        s_ya = sem("y_ready")
        s_out = sem("out_stored")

        block = ctx.enter_context(nc.Block())

        ZEROED = 6
        W_DMAS = 2 * GK + 2

        def weight(layer, tile, many=None):
            split = (layer, tile) in SPLIT_TILES
            at = (SPLIT_TILES if split else PLAIN_TILES).index((layer, tile))
            where = w_stage if split else w_plain[:]
            return where[:, at, :] if many is None else where[:, at:at + many, :]

        def make_low(engine, name, t, c, k):
            layer, tiles = group_tiles(k)
            rows, slot, many = (ROWS0 if layer == 0 else P), hl_slot(c, k), len(tiles)
            engine.wait_ge(s_high, made(t, c, k, SPLIT_ORDER))
            engine.tensor_tensor(low[0:rows, slot, 0:many, :], prod[0:rows, k % RING, 0:many, :],
                                 high[0:rows, slot, 0:many, :].bitcast(F32), ALU.subtract).then_inc(s_low[name], 1)

        def number(t, c, k):
            return t * (PER * CPB) + ((c + 1) * PER + k)

        def made(t, c, k, among):
            return t * (len(among) * CPB) + ((c + 1) * len(among) + sum(x <= k for x in among))

        BY = {e: [k for k in SPLIT_ORDER if SPLIT[k] == e] for e in ("dve", "pool")}

        def hl_slot(c, k):
            return ((c + 1) * len(SPLIT_ORDER) + SPLIT_ORDER.index(k)) % HL

        def count_phantoms(engine, own, members, ks, t=0, c=-1):
            here = [k for k in ks if k in members]
            if here:
                before = made(t, c, here[0] - 1, members)
                if before:
                    engine.wait_ge(own, before)
                engine.sem_inc(own, len(here))

        ALL = list(range(PER))
        AHEAD, ZERO, BEHIND = ALL[:K0], ALL[K0:K2], ALL[K2:]
        LAST = (BLOCKS - 1, CPB - 1)

        def is_last(t, c):
            return isinstance(t, int) and (t, c) == LAST

        @block.sync
        def _(sp):
            sp.dma_start(ids_sb[:], ids.rearrange("(t p) f -> p t f", p=P)).then_inc(s_ids, 16)
            sp.dma_start(eye_sb[:], eye).then_inc(s_eye, 16)
            sp.wait_ge(s_zeroed, 1)
            for j in range(SHIFTS):
                tile, p0 = j // JT, (j % JT) * FIELDS
                for wrap, lo, hi in ((0, 0, FIELDS - j), (1, FIELDS - j, FIELDS)):
                    if lo == hi:
                        continue
                    k0 = lo + j - wrap * FIELDS
                    step = [[(FIELDS + 1) * S, hi - lo], [1, S]]
                    sp.dma_start(weight(0, tile)[p0 + lo:p0 + hi, :],
                                 bass.AP(w0.tensor, (lo * FIELDS + k0) * S, step)).then_inc(s_w0, 16)
                    if j:
                        sp.dma_start(w0_swapped[p0 + lo:p0 + hi, tile, :],
                                     bass.AP(w0.tensor, (k0 * FIELDS + lo) * S, step)).then_inc(s_w0, 16)

            def store_x0(t):
                sp.wait_ge(s_turned, t * CPB + CPB)
                for copy in range(2):
                    rows = slice(copy * FIELDS, (copy + 1) * FIELDS)
                    sp.dma_start(x0_rows[rows, bass.ds(t * BLOCK_N, BLOCK_N)], x0_t[:]).then_inc(s_x0, 16)

            def load_pair0(n0):
                for jj in range(JT):
                    rows = slice(jj * FIELDS, (jj + 1) * FIELDS)
                    tiles = T0 if jj * FIELDS < LAST0 else T0 - 1
                    sp.dma_start(pair0[rows, 0:tiles, :],
                                 bass.AP(x0_rows, n0 + jj * N, [[N, FIELDS], [JT * N, tiles], [1, CH]])
                                 ).then_inc(s_pair0, 16)
                    sp.dma_start(pair0[rows, T0, :],
                                 bass.AP(x0_rows, n0, [[N, FIELDS], [1, CH]])).then_inc(s_pair0, 16)

            def load_xh(dst, tile, n0, done):
                for odd in range(2):
                    tiles = min(dst.shape[1], (FIELDS - odd + 1) // 2 - tile)
                    sp.dma_start(dst[odd * HALF:(odd + 1) * HALF, 0:tiles, :],
                                 bass.AP(x0_rows, n0 + (2 * tile + odd) * N, [[0, HALF], [2 * N, tiles], [1, CH]])
                                 ).then_inc(done, 16)

            def load_back(g, n0):
                load_xh(xh_back[:, g * GT:(g + 1) * GT, :], (FRONT + g) * GT, n0, s_back[g])

            store_x0(0)
            sp.wait_ge(s_x0, 32)
            sp.wait_ge(s_zeroed, ZEROED)
            load_pair0(0)
            load_xh(xh_front[:, 0], 0, 0, s_front[0])
            for g in range(BACK):
                load_back(g, 0)

            def step(t, c):
                n0 = t * BLOCK_N + (c + 1) * CH
                if c == 2 and not isinstance(t, int):
                    store_x0(t + 1)
                if c == CPB - 1:
                    sp.wait_ge(s_x0, t * 32 + 64)
                sp.wait_ge(s_prod, number(t, c, 0))
                load_pair0(n0)
                load_xh(xh_front[:, (c + 1) % 2], 0, n0, s_front[(c + 1) % 2])
                for g in range(BACK):
                    sp.wait_ge(s_prod, number(t, c, K2 + FRONT + g + 1))
                    load_back(g, n0)

            with sp.Fori(0, BLOCKS - 1) as t:
                for c in range(CPB):
                    step(t, c)
            for c in range(CPB - 1):
                step(BLOCKS - 1, c)
            sp.dma_start(wt1_sb, wt1[0:2 * P, :].rearrange("(k p) m -> p k m", p=P)).then_inc(s_top, 16)
            sp.dma_start(wt1d_sb, wt1[2 * P:2 * P + D, :]).then_inc(s_top, 16)
            sp.dma_start(wt2_sb, wt2.rearrange("(k p) m -> p k m", p=P)).then_inc(s_top, 16)
            sp.wait_ge(s_ya, B // CH)
            sp.dma_start(out.rearrange("b o -> o b"), y_sb).then_inc(s_out, 16)
            sp.wait_ge(s_out, 16)

        @block.gpsimd
        def _(pool):
            def copy_ids(t):
                pool.tensor_copy(ids_cur[:], ids_sb[:, bass.ds(t, 1), :]).then_inc(s_idcur, 1)
                pool.wait_ge(s_idcur, t + 1)
                pool.sem_inc(s_blocks, 1)

            def gather(fields):
                for f in fields:
                    pool.indirect_dma_start(emb[:, f, :], None, tables[f],
                                            bass.IndirectOffsetOnAxis(ap=ids_cur[:, f:f + 1], axis=0)
                                            ).then_inc(s_gather, 16)

            pool.wait_ge(s_ids, 16)
            copy_ids(0)
            gather(range(FIELDS))
            count_phantoms(pool, s_low["pool"], BY["pool"], AHEAD)
            for k in ZERO:
                if k in BY["pool"]:
                    make_low(pool, "pool", 0, -1, k)
            count_phantoms(pool, s_low["pool"], BY["pool"], BEHIND)
            pool.wait_ge(s_gather, 16 * FIELDS)
            pool.wait_ge(s_turn, CPB)
            copy_ids(1)
            gather(range(FIELDS))

            def step(t, c, gathering):
                lows = [k for k in BY["pool"] if not is_last(t, c) or k not in ZERO]
                todo = list(range(FIELDS))[(c - 1) * FIELDS // 3:c * FIELDS // 3] if gathering and c else []
                for n, k in enumerate(lows):
                    make_low(pool, "pool", t, c, k)
                    if n == 0 and c == 1 and gathering:
                        pool.wait_ge(s_gather, t * (16 * FIELDS) + 2 * 16 * FIELDS)
                        pool.wait_ge(s_turn, t * CPB + 2 * CPB)
                        copy_ids(t + 2)
                    gather(todo[sum(LOOKUPS[:n]):sum(LOOKUPS[:n + 1])])
                    if is_last(t, c) and k == max(x for x in BY["pool"] if x < K0):
                        count_phantoms(pool, s_low["pool"], BY["pool"], ZERO, *LAST)

            with pool.Fori(0, BLOCKS - 2) as t:
                for c in range(CPB):
                    step(t, c, True)
            for t in (BLOCKS - 2, BLOCKS - 1):
                for c in range(CPB):
                    step(t, c, False)

        @block.scalar
        def _(act):
            act.wait_ge(s_zeroed, 1)
            for k in [*AHEAD, *BEHIND]:
                layer, tiles = group_tiles(k)
                w = (w1, w2)[layer - 1].rearrange("h k s -> (h k) s")
                whole = [n for n in tiles if n < TK - 1]
                act.dma_start(weight(layer, tiles[0], len(whole)),
                              w[tiles[0] * P:(whole[-1] + 1) * P, :].rearrange("(t p) s -> p t s", p=P)
                              ).then_inc(s_w, 16)
                if tiles[-1] == TK - 1:
                    act.dma_start(weight(layer, TK - 1)[0:HALF, :], w[(TK - 1) * P:, :]).then_inc(s_w, 16)
            for n, b in enumerate((b0, b1, b2)):
                act.dma_start(bias_sb[:, n:n + 1], b.rearrange("(s o) -> s o", o=1)).then_inc(s_small, 16)
            act.dma_start(bt1_sb[:], bt1.rearrange("(m p) -> p m", p=P), allow_slow_non_contiguous=True
                          ).then_inc(s_small, 16)
            act.dma_start(bt2_sb[:], bt2.rearrange("(m p) -> p m", p=P), allow_slow_non_contiguous=True
                          ).then_inc(s_small, 16)
            act.dma_start(wt3_sb[:], wt3.rearrange("(k p) o -> p k o", p=P), allow_slow_non_contiguous=True
                          ).then_inc(s_small, 16)
            act.dma_start(dense_sb[:], dense.rearrange("(t p) c -> p t c", p=P)).then_inc(s_small, 16)
            act.sem_inc(s_act[1], 1)

            act.wait_ge(s_w, 16 * W_DMAS)
            act.wait_ge(s_w0sum, 1)
            act.activation(w_high[:], w_stage, ACT.Copy).then_inc(s_whigh, 1)

            def evacuate_turn(t, r):
                act.wait_ge(s_turn, t * CPB + (r + 1))
                act.activation(x0_t[:, r * CH:(r + 1) * CH], turn[r % 2][0:FIELDS, :], ACT.Copy).then_inc(s_turned, 1)

            def relu(dst, layer, lo, hi):
                return act.activation(dst, z[layer][lo:hi, :], ACT.Relu, bias=bias_sb[lo:hi, layer:layer + 1])

            def activate0(slot):
                relu(xk[1][0:HALF, :], 0, 0, HALF)
                relu(xk[1][HALF:S, :], 0, 0, HALF).then_inc(s_xk[1], 1)
                relu(direct01[0:HALF, slot, :], 0, HALF, S).then_inc(s_act[0], 1)

            def make_highs(t, c, ks):
                for k in ks:
                    if k not in SPLIT:
                        continue
                    layer, tiles = group_tiles(k)
                    rows, slot = (ROWS0 if layer == 0 else P), hl_slot(c, k)
                    back = SPLIT_ORDER.index(k) - HL
                    before = SPLIT_ORDER[back % len(SPLIT_ORDER)] + (back // len(SPLIT_ORDER)) * PER
                    if number(0, c, before) >= 0:
                        act.wait_ge(s_summed, number(t, c, before + 1))
                    act.wait_ge(s_prod, number(t, c, k + 1))
                    act.activation(high[0:rows, slot, 0:len(tiles), :], prod[0:rows, k % RING, 0:len(tiles), :],
                                   ACT.Copy).then_inc(s_high, 1)

            for r in range(CPB):
                evacuate_turn(0, r)
            act.wait_ge(s_zeroed, ZEROED)
            act.wait_ge(s_small, 7 * 16)
            count_phantoms(act, s_high, SPLIT_ORDER, AHEAD)
            make_highs(0, -1, ZERO)
            count_phantoms(act, s_high, SPLIT_ORDER, BEHIND)
            act.wait_ge(s_summed, number(0, -1, K2))
            activate0(0)

            def step(t, c):
                last = is_last(t, c)
                make_highs(t, c, AHEAD)
                act.wait_ge(s_summed, number(t, c, 0))
                if c % 2:
                    act.wait_ge(s_red2, t * 2 + (c + 1) // 2)
                relu(direct2[:, (c + 1) % 2, :], 2, 0, S).then_inc(s_act[2], 1)
                if c == 1 and not isinstance(t, int):
                    evacuate_turn(t + 1, 2)
                    evacuate_turn(t + 1, 3)
                if not last:
                    make_highs(t, c, ZERO)
                act.wait_ge(s_summed, number(t, c, K0))
                act.wait_ge(s_prod, number(t, c, 0))
                relu(xk[2][0:HALF, :], 1, 0, HALF)
                relu(xk[2][HALF:S, :], 1, 0, HALF).then_inc(s_xk[2], 1)
                relu(direct01[HALF:S, c % 2, :], 1, HALF, S).then_inc(s_act[1], 1)
                if c == 0 and not isinstance(t, int):
                    act.wait_ge(s_x0, t * 32 + 32)
                    evacuate_turn(t + 1, 0)
                    evacuate_turn(t + 1, 1)
                if not last:
                    act.wait_ge(s_summed, number(t, c, K2))
                    act.wait_ge(s_prod, number(t, c, K0))
                    if c % 2:
                        act.wait_ge(s_red01, t * 2 + (c + 1) // 2)
                    activate0((c + 1) % 2)
                else:
                    count_phantoms(act, s_high, SPLIT_ORDER, ZERO, *LAST)
                make_highs(t, c, BEHIND)

            with act.Fori(0, BLOCKS - 1) as t:
                for c in range(CPB):
                    step(t, c)
            for c in range(CPB):
                step(BLOCKS - 1, c)
            act.wait_ge(s_summed, number(*LAST, PER))
            act.wait_ge(s_red2, 2 * BLOCKS)
            relu(direct2[:, 1, :], 2, 0, S).then_inc(s_act[2], 1)

            for r in range(B // CH):
                act.wait_ge(s_dt, r + 1)
                act.activation(dense_t[:, r, :], turn[r % 2][0:D, :], ACT.Copy).then_inc(s_dte, 1)
            for q in range(B // CH):
                for m in range(M1):
                    act.wait_ge(s_h1, q * M1 + m + 1)
                    if q:
                        act.wait_ge(s_h2, q * M2)
                    act.activation(h1[:, m, :], z[m % 2][:], ACT.Relu, bias=bt1_sb[:, m:m + 1]).then_inc(s_h1a, 1)
                for m in range(M2):
                    act.wait_ge(s_h2, q * M2 + m + 1)
                    if q:
                        act.wait_ge(s_y, q)
                    act.activation(h2[:, m, :], xk[1 + m][:], ACT.Relu, bias=bt2_sb[:, m:m + 1]).then_inc(s_h2a, 1)
                act.wait_ge(s_y, q + 1)
                act.activation(y_sb[:, q * CH:(q + 1) * CH], z[2][0:1, :], ACT.Copy).then_inc(s_ya, 1)

        @block.vector
        def _(dve):
            dve.memset(stage, 0.0).then_inc(s_zeroed, 1)
            dve.memset(pair0[0:ROWS0, T0 - 1, :], 0.0).then_inc(s_zeroed, 1)
            dve.memset(xh_back[HALF:S, BACK * GT - 1, :], 0.0).then_inc(s_zeroed, 1)
            dve.memset(direct2[:], 0.0).then_inc(s_zeroed, 1)
            dve.memset(z[2][:], 0.0).then_inc(s_zeroed, 1)
            dve.memset(part2[:], 0.0).then_inc(s_zeroed, 1)
            dve.wait_ge(s_w0, 16 * (4 * (SHIFTS - 1) + 1))
            for n, k in enumerate(ZERO):
                tiles = group_tiles(k)[1]
                if k in SPLIT or tiles[-1] < T0 - 1:
                    pieces = [(ROWS0, tiles[0], len(tiles))]
                else:
                    pieces = [(ROWS0, tiles[0], len(tiles) - 1), (LAST0, T0 - 1, 1)]
                for rows, tile, many in pieces:
                    w = weight(0, tile, many)[0:rows]
                    ins = dve.tensor_tensor(w, w, w0_swapped[0:rows, tile:tile + many, :], ALU.add)
            ins.then_inc(s_w0sum, 1)
            dve.wait_ge(s_whigh, 1)
            dve.tensor_tensor(w_low[:], w_stage, w_high[:].bitcast(F32), ALU.subtract).then_inc(s_wlow, 1)
            dve.wait_ge(s_wlow, 1)

            def multiply(t, c, k, first):
                layer, tiles = group_tiles(k)
                many = len(tiles)
                if layer == 0:
                    rows, one, other = ROWS0, pair0[0:ROWS0, tiles[0]:tiles[0] + many, :], pair0[0:ROWS0, T0, :]
                else:
                    rows, other = P, xk[layer][:]
                    if tiles[0] < FRONT * GT:
                        one = xh_front[:, c % 2, tiles[0]:tiles[0] + many, :]
                    else:
                        at = tiles[0] - FRONT * GT
                        one = xh_back[:, at:at + many, :]
                        if layer == 1:
                            dve.wait_ge(s_back[at // GT], t * (32 * CPB) + (c + 1) * 32)
                if not first:
                    before = k - RING
                    kind = SPLIT.get(before % PER)
                    if kind:
                        b = c + before // PER
                        dve.wait_ge(s_low[kind], made(t, b, before % PER, BY[kind]))
                    else:
                        dve.wait_ge(s_summed, number(t, c, before + 1))
                dve.tensor_tensor(prod[0:rows, k % RING, 0:many, :], one,
                                  other.unsqueeze(1).broadcast_to([rows, many, CH]), ALU.mult).then_inc(s_prod, 1)

            pending = []

            def products(t, c, ks, first=False):
                for k in ks:
                    multiply(t, c, k, first)
                    flush()
                    if k in BY["dve"]:
                        pending.append((t, c, k))

            def flush():
                while pending:
                    make_low(dve, "dve", *pending.pop())

            def reduce(dst, src, done):
                dve.tensor_reduce(dst, src[:].rearrange("p s (d b) -> p b (s d)", b=P), AX_X, ALU.add).then_inc(done, 1)

            def layer1(t, c):
                dve.wait_ge(s_xk[1], t * CPB + (c + 1))
                dve.wait_ge(s_front[c % 2], t * (32 * CPB // 2) + (c // 2 + 1) * 32)
                products(t, c, AHEAD)

            count_phantoms(dve, s_prod, ALL, AHEAD)
            count_phantoms(dve, s_low["dve"], BY["dve"], AHEAD)
            dve.wait_ge(s_pair0, 16 * 2 * JT)
            products(0, -1, ZERO, first=True)
            flush()
            count_phantoms(dve, s_prod, ALL, BEHIND)
            count_phantoms(dve, s_low["dve"], BY["dve"], BEHIND)
            layer1(0, 0)
            flush()

            def step(t, c):
                chunk = t * CPB + c
                last = is_last(t, c)
                if last:
                    count_phantoms(dve, s_prod, ALL, ZERO, *LAST)
                    count_phantoms(dve, s_low["dve"], BY["dve"], ZERO, *LAST)
                else:
                    dve.wait_ge(s_pair0, chunk * (16 * 2 * JT) + 2 * 16 * 2 * JT)
                    products(t, c, ZERO)
                    flush()
                if c == 0:
                    dve.wait_ge(s_act[2], chunk + 1)
                    reduce(part2[:, 1, :], direct2, s_red2)
                    dve.wait_ge(s_red2, t * 2 + 1)
                    dve.tensor_tensor(sum2[:, bass.ds(t, 1), :], part2[:, 0:1, :], part2[:, 1:2, :],
                                      ALU.add).then_inc(s_sum2, 1)
                if c == 2:
                    dve.wait_ge(s_act[2], chunk + 1)
                    reduce(part2[:, 0, :], direct2, s_red2)
                dve.wait_ge(s_xk[2], chunk + 1)
                products(t, c, BEHIND[:2])
                if c % 2:
                    dve.wait_ge(s_act[1], chunk + 2)
                    reduce(part01[:, c // 2, :], direct01, s_red01)
                products(t, c, BEHIND[2:])
                if not last:
                    layer1(t, c + 1)
                flush()
                if c == CPB - 1:
                    dve.wait_ge(s_red01, t * 2 + 2)
                    dve.tensor_tensor(sum01[:, bass.ds(t, 1), :], part01[:, 0:1, :], part01[:, 1:2, :],
                                      ALU.add).then_inc(s_sum01, 1)

            with dve.Fori(0, BLOCKS - 1) as t:
                for c in range(CPB):
                    step(t, c)
            for c in range(CPB):
                step(BLOCKS - 1, c)
            dve.wait_ge(s_act[2], CHUNKS + 1)
            reduce(part2[:, 1, :], direct2, s_red2)
            dve.wait_ge(s_red2, 2 * BLOCKS + 1)
            dve.tensor_tensor(sum2[:, BLOCKS, :], part2[:, 0, :], part2[:, 1, :], ALU.add).then_inc(s_sum2, 1)

        @block.tensor
        def _(pe):
            def turn_round(r):
                for q in range(DC):
                    mm = pe.transpose(turn[r % 2][0:FIELDS, q * P:(q + 1) * P], emb[:, :, r * DC + q], eye_sb[:])
                mm.then_inc(s_turn, 1)

            def sum_groups(t, c, ks):
                for k in ks:
                    layer, tiles = group_tiles(k)
                    first, last = k == ks[0], k == ks[-1]
                    jobs = [(n, tile, tile_rows(layer, tile)) for n, tile in enumerate(tiles)]
                    if k not in SPLIT:
                        pe.wait_ge(s_prod, number(t, c, k + 1))
                        for n, tile, rows in jobs:
                            mm = pe.matmul(z[layer][:], weight(layer, tile)[0:rows, :], prod[0:rows, k % RING, n, :],
                                           start=first and n == 0, stop=last and n == len(tiles) - 1)
                        mm.then_inc(s_summed, 1)
                        continue
                    slot = hl_slot(c, k)
                    pe.wait_ge(s_high, made(t, c, k, SPLIT_ORDER))
                    for w in (w_high, w_low):
                        for n, tile, rows in jobs:
                            pe.matmul(z[layer][:], w[0:rows, SPLIT_TILES.index((layer, tile)), :],
                                      high[0:rows, slot, n, :], start=first and n == 0 and w is w_high, stop=False)
                    pe.wait_ge(s_low[SPLIT[k]], made(t, c, k, BY[SPLIT[k]]))
                    for n, tile, rows in jobs:
                        mm = pe.matmul(z[layer][:], w_high[0:rows, SPLIT_TILES.index((layer, tile)), :],
                                       low[0:rows, slot, n, :], start=False, stop=last and n == len(tiles) - 1)
                    mm.then_inc(s_summed, 1)

            pe.wait_ge(s_eye, 16)
            pe.wait_ge(s_gather, 16 * FIELDS)
            for r in range(CPB):
                if r >= 2:
                    pe.wait_ge(s_turned, r - 1)
                turn_round(r)
            pe.wait_ge(s_wlow, 1)
            count_phantoms(pe, s_summed, ALL, AHEAD)
            sum_groups(0, -1, ZERO)
            count_phantoms(pe, s_summed, ALL, BEHIND)

            def step(t, c):
                chunk = t * CPB + c
                last = is_last(t, c)
                turns = c == 0 and not isinstance(t, int)
                if turns:
                    pe.wait_ge(s_gather, t * (16 * FIELDS) + 2 * 16 * FIELDS)
                    pe.wait_ge(s_turned, t * CPB + CPB)
                pe.wait_ge(s_act[1], chunk + 1)
                sum_groups(t, c, AHEAD)
                if turns:
                    turn_round(0)
                    turn_round(1)
                if last:
                    count_phantoms(pe, s_summed, ALL, ZERO, *LAST)
                else:
                    pe.wait_ge(s_act[0], chunk + 1)
                    sum_groups(t, c, ZERO)
                if turns:
                    pe.wait_ge(s_turned, t * CPB + (CPB + 2))
                pe.wait_ge(s_act[2], chunk + 1)
                sum_groups(t, c, BEHIND)
                if turns:
                    turn_round(2)
                    turn_round(3)

            with pe.Fori(0, BLOCKS - 1) as t:
                for c in range(CPB):
                    step(t, c)
            for c in range(CPB):
                step(BLOCKS - 1, c)

            pe.wait_ge(s_small, 7 * 16)
            for r in range(B // CH):
                if r >= 2:
                    pe.wait_ge(s_dte, r - 1)
                for q in range(DC):
                    mm = pe.transpose(turn[r % 2][0:D, q * P:(q + 1) * P], dense_sb[:, r * DC + q, :], eye_sb[:])
                mm.then_inc(s_dt, 1)
            pe.wait_ge(s_top, 3 * 16)
            pe.wait_ge(s_sum01, BLOCKS)
            pe.wait_ge(s_sum2, BLOCKS + 1)
            pe.wait_ge(s_act[2], CHUNKS + 1)
            for q in range(B // CH):
                blocks = slice(q * DC, (q + 1) * DC)
                cin2 = slice(q * DC + 1, (q + 1) * DC + 1)
                pe.wait_ge(s_dte, q + 1)
                for m in range(M1):
                    if q * M1 + m >= 2:
                        pe.wait_ge(s_h1a, q * M1 + m - 1)
                    cols = slice(m * P, (m + 1) * P)
                    pe.matmul(z[m % 2][:], wt1_sb[:, 0, cols],
                              sum01[:, blocks, :].rearrange("p t b -> p (t b)"), start=True, stop=False)
                    pe.matmul(z[m % 2][:], wt1_sb[:, 1, cols],
                              sum2[:, cin2, :].rearrange("p t b -> p (t b)"), start=False, stop=False)
                    pe.matmul(z[m % 2][:], wt1d_sb[:, cols], dense_t[:, q, :],
                              start=False, stop=True).then_inc(s_h1, 1)
                for m in range(M2):
                    if q:
                        pe.wait_ge(s_h2a, q * M2 - M2 + m + 1)
                    for k in range(M1):
                        pe.wait_ge(s_h1a, q * M1 + k + 1)
                        mm = pe.matmul(xk[1 + m][:], wt2_sb[:, k, m * P:(m + 1) * P], h1[:, k, :],
                                       start=k == 0, stop=k == M1 - 1)
                    mm.then_inc(s_h2, 1)
                if q:
                    pe.wait_ge(s_ya, q)
                pe.wait_ge(s_h2a, (q + 1) * M2)
                for k in range(M2):
                    mm = pe.matmul(z[2][0:1, :], wt3_sb[:, k, :], h2[:, k, :], start=k == 0, stop=k == M2 - 1)
                mm.then_inc(s_y, 1)


_TABLES = [f"tbl_{f}" for f in range(FIELDS)]
_INS = ["dense_ctx", "ids", *_TABLES, "L0_rec_w0", "L0_rec_w1", "L0_rec_w2", "L0_rec_b0", "L0_rec_b1",
        "L0_rec_b2", "W_top1", "b_top1", "W_top2", "b_top2", "W_top3"]


def kernel(**inputs):
    import numpy as np
    import concourse.bacc as bacc
    from concourse.bass_utils import run_bass_kernel_spmd

    nc = bacc.Bacc("TRN2", target_bir_lowering=False, num_devices=1)
    arrays, aps = {}, {}
    for name in _INS:
        a = np.ascontiguousarray(inputs[name])
        arrays[f"in_{name}_dram"] = a
        aps[name] = nc.dram_tensor(f"in_{name}_dram", a.shape, mybir.dt.from_np(a.dtype), kind="ExternalInput").ap()
    arrays["in_eye_dram"] = np.eye(P, dtype=np.float32)
    eye = nc.dram_tensor("in_eye_dram", (P, P), F32, kind="ExternalInput").ap()
    out = nc.dram_tensor("out_0_dram", (inputs["ids"].shape[0], 1), F32, kind="ExternalOutput").ap()
    rest = [aps[name] for name in _INS[2 + FIELDS:]]
    build(nc, aps["dense_ctx"], aps["ids"], [aps[name] for name in _TABLES], *rest, eye, out)
    r = run_bass_kernel_spmd(nc, [arrays], core_ids=[0])
    return r.results[0]["out_0_dram"]
```

```python
from contextlib import ExitStack

import concourse.bass as bass
from concourse import mybir

F32 = mybir.dt.float32
F32R = mybir.dt.float32r
I32 = mybir.dt.int32
ALU = mybir.AluOpType
ACT = mybir.ActivationFunctionType
AX_X = mybir.AxisListType.X

P = 128
FIELDS = 39
D = 16
S = 128
HALF = S // 2
CH = 512
DC = CH // P
CPB = D // DC
GT = 4
RING = 4

SHIFTS = FIELDS // 2 + 1
JT = 3
T0 = -(-SHIFTS // JT)
ROWS0 = JT * FIELDS
LAST0 = (SHIFTS - JT * (T0 - 1)) * FIELDS
TK = -(-FIELDS // 2)
GK = TK // GT
FRONT = 1
BACK = GK - FRONT
G0 = [range(0, GT), range(GT, T0)]
PER = 2 * GK + len(G0)
K0 = GK
K2 = GK + len(G0)
SPLIT = {1: "dve", 2: "pool", 3: "dve", 4: "dve", 10: "pool", 11: "dve"}
HIGHS = 3
LOWS = 2
TWICE = 2 * FIELDS
THIRD = FIELDS // 3
LOOKUPS = (THIRD, 0)


def group_tiles(k):
    if k < K0:
        return 1, range(k * GT, (k + 1) * GT)
    if k < K2:
        return 0, G0[k - K0]
    return 2, range((k - K2) * GT, (k - K2 + 1) * GT)


SPLIT_TILES = [(group_tiles(k)[0], n) for k in range(PER) if k in SPLIT for n in group_tiles(k)[1]]
PLAIN_TILES = [(group_tiles(k)[0], n) for k in range(PER) if k not in SPLIT for n in group_tiles(k)[1]]
SPLIT_ORDER = sorted(SPLIT)


def tile_rows(layer, tile):
    if layer == 0:
        return LAST0 if tile == T0 - 1 else ROWS0
    return HALF if tile == TK - 1 else P


def build(nc, dense, ids, tables, w0, w1, w2, b0, b1, b2, wt1, bt1, wt2, bt2, wt3, eye, out):
    B = ids.shape[0]
    BLOCKS = B // P
    N = B * D
    BLOCK_N = P * D
    CHUNKS = BLOCKS * CPB
    H1 = wt1.shape[1]
    H2 = wt2.shape[1]
    M1, M2 = H1 // P, H2 // P
    assert w0.shape == (FIELDS, FIELDS, S) and GK * GT == TK and CPB == 4 and B % CH == 0
    assert not any(K0 <= k < K2 for k in SPLIT) and FIELDS % 3 == 0
    assert PER % RING == 0 and CPB * len(SPLIT) % HIGHS == 0 and CPB * len(SPLIT) % LOWS == 0

    ctx = ExitStack()
    with ctx:
        def sb(name, shape, dt=F32):
            return ctx.enter_context(nc.sbuf_tensor(name, shape, dt))

        def bank(name):
            return ctx.enter_context(nc.psum_tensor(name, [P, CH], F32))

        def sem(name):
            return ctx.enter_context(nc.semaphore(name))

        x0_rows = nc.dram_tensor("x0_rows", (TWICE, N), F32, kind="Internal")

        w_plain = sb("w_plain", [P, len(PLAIN_TILES), S])
        w_high = sb("w_high", [P, len(SPLIT_TILES), S], F32R)
        w_low = sb("w_low", [P, len(SPLIT_TILES), S], F32R)
        bias_sb = sb("bias_sb", [P, 3])
        eye_sb = sb("eye_sb", [P, P])
        ids_sb = sb("ids_sb", [P, BLOCKS, FIELDS], I32)
        ids_cur = sb("ids_cur", [P, FIELDS], I32)
        emb = sb("emb", [P, FIELDS, D])
        x0_t = sb("x0_t", [FIELDS, BLOCK_N // 2])
        pair0 = sb("pair0", [P, T0 + 1, CH])
        xh_front = sb("xh_front", [P, 2, FRONT * GT, CH])
        xh_back = sb("xh_back", [P, BACK * GT, CH])
        prod = sb("prod", [P, RING, GT, CH])
        high = sb("high", [P, HIGHS, GT, CH], F32R)
        low = sb("low", [P, LOWS, GT, CH], F32R)
        direct01 = sb("direct01", [P, 2, CH])
        direct2 = sb("direct2", [P, 2, CH])
        part01 = sb("part01", [P, 2, P])
        part2 = sb("part2", [P, 2, P])
        sum01 = sb("sum01", [P, BLOCKS, P])
        sum2 = sb("sum2", [P, BLOCKS + 1, P])
        bt1_sb = sb("bt1_sb", [P, M1])
        bt2_sb = sb("bt2_sb", [P, M2])
        wt3_sb = sb("wt3_sb", [P, M2, 1])
        stage = prod[:].rearrange("p r g n -> p (r g n)").rearrange("p (t s) -> p t s", s=S)
        w_stage = stage[:, 0:len(SPLIT_TILES), :]
        w0_swapped = stage[:, len(SPLIT_TILES):len(SPLIT_TILES) + T0, :]
        wt1_sb = xh_front[:, 0, 0:2, :]
        wt1d_sb = xh_front[0:D, 0, 2, :]
        wt2_sb = pair0[:, 0:2, :].rearrange("p a n -> p (a n)").rearrange("p (k m) -> p k m", k=M1)
        dense_t = xh_back[0:D, 0:B // CH, :]
        h1 = xh_back[:, 4:4 + M1, :]
        h2 = xh_back[:, 8:8 + M2, :]
        dense_sb = pair0[:, 2, 0:BLOCKS * D].rearrange("p (t c) -> p t c", c=D)
        y_sb = xh_front[0:1, 1].rearrange("p a n -> p (a n)")

        z = [bank(f"z{layer}") for layer in range(3)]
        xk = [None, bank("xk1"), bank("xk2")]
        turn = [bank("turn0"), bank("turn1")]

        s_ids = sem("ids_loaded")
        s_eye = sem("eye_loaded")
        s_w0 = sem("w0_loaded")
        s_w = sem("w12_loaded")
        s_small = sem("small_loaded")
        s_zeroed = sem("zeroed")
        s_w0sum = sem("w0_summed")
        s_whigh = sem("w_high_ready")
        s_wlow = sem("w_low_ready")
        s_idcur = sem("ids_copied")
        s_blocks = sem("blocks_begun")
        s_gather = sem("gathered")
        s_turn = sem("turned")
        s_turned = sem("turn_evacuated")
        s_x0 = sem("x0_stored")
        s_pair0 = sem("pair0_loaded")
        s_front = [sem("xh_front_loaded0"), sem("xh_front_loaded1")]
        s_back = [sem(f"xh_back_loaded{g}") for g in range(BACK)]
        s_xk = [None, sem("xk1_ready"), sem("xk2_ready")]
        s_prod = sem("products_made")
        s_high = sem("highs_made")
        s_low = {"dve": sem("lows_made_dve"), "pool": sem("lows_made_pool")}
        s_summed = sem("groups_summed")
        s_act = [sem(f"layer{layer}_activated") for layer in range(3)]
        s_red01 = sem("direct01_reduced")
        s_red2 = sem("direct2_reduced")
        s_sum01 = sem("sum01_ready")
        s_sum2 = sem("sum2_ready")
        s_top = sem("top_weights_loaded")
        s_dt = sem("dense_turned")
        s_dte = sem("dense_t_ready")
        s_h1 = sem("h1_products")
        s_h1a = sem("h1_ready")
        s_h2 = sem("h2_products")
        s_h2a = sem("h2_ready")
        s_y = sem("y_products")
        s_ya = sem("y_ready")
        s_out = sem("out_stored")

        block = ctx.enter_context(nc.Block())

        ZEROED = 6
        W_DMAS = 2 * GK + 2

        def weight(layer, tile, many=None):
            split = (layer, tile) in SPLIT_TILES
            at = (SPLIT_TILES if split else PLAIN_TILES).index((layer, tile))
            where = w_stage if split else w_plain[:]
            return where[:, at, :] if many is None else where[:, at:at + many, :]

        def make_low(engine, name, t, c, k):
            layer, tiles = group_tiles(k)
            rows, many = (ROWS0 if layer == 0 else P), len(tiles)
            wait_slot(engine, t, c, k, LOWS)
            engine.wait_ge(s_high, made(t, c, k, SPLIT_ORDER))
            engine.tensor_tensor(low[0:rows, slot(c, k, LOWS), 0:many, :], prod[0:rows, k % RING, 0:many, :],
                                 high[0:rows, slot(c, k, HIGHS), 0:many, :].bitcast(F32),
                                 ALU.subtract).then_inc(s_low[name], 1)

        def number(t, c, k):
            return t * (PER * CPB) + ((c + 1) * PER + k)

        def made(t, c, k, among):
            return t * (len(among) * CPB) + ((c + 1) * len(among) + sum(x <= k for x in among))

        BY = {e: [k for k in SPLIT_ORDER if SPLIT[k] == e] for e in ("dve", "pool")}

        def slot(c, k, slots):
            return ((c + 1) * len(SPLIT_ORDER) + SPLIT_ORDER.index(k)) % slots

        def wait_slot(engine, t, c, k, slots):
            back = SPLIT_ORDER.index(k) - slots
            before = SPLIT_ORDER[back % len(SPLIT_ORDER)] + (back // len(SPLIT_ORDER)) * PER
            if number(0, c, before) >= 0:
                engine.wait_ge(s_summed, number(t, c, before + 1))

        def count_phantoms(engine, own, members, ks, t=0, c=-1):
            here = [k for k in ks if k in members]
            if here:
                before = made(t, c, here[0] - 1, members)
                if before:
                    engine.wait_ge(own, before)
                engine.sem_inc(own, len(here))

        ALL = list(range(PER))
        AHEAD, ZERO, BEHIND = ALL[:K0], ALL[K0:K2], ALL[K2:]
        LAST = (BLOCKS - 1, CPB - 1)

        def is_last(t, c):
            return isinstance(t, int) and (t, c) == LAST

        @block.sync
        def _(sp):
            sp.dma_start(ids_sb[:], ids.rearrange("(t p) f -> p t f", p=P)).then_inc(s_ids, 16)
            sp.dma_start(eye_sb[:], eye).then_inc(s_eye, 16)
            for j in range(SHIFTS):
                tile, p0 = j // JT, (j % JT) * FIELDS
                for wrap, lo, hi in ((0, 0, FIELDS - j), (1, FIELDS - j, FIELDS)):
                    if lo == hi:
                        continue
                    k0 = lo + j - wrap * FIELDS
                    sp.dma_start(weight(0, tile)[p0 + lo:p0 + hi, :],
                                 bass.AP(w0.tensor, (lo * FIELDS + k0) * S, [[(FIELDS + 1) * S, hi - lo], [1, S]])
                                 ).then_inc(s_w0, 16)

            def store_x0(t, half):
                sp.wait_ge(s_turned, t * CPB + (half + 1) * 2)
                for copy in range(2):
                    rows = slice(copy * FIELDS, (copy + 1) * FIELDS)
                    sp.dma_start(x0_rows[rows, bass.ds(t * BLOCK_N + half * (BLOCK_N // 2), BLOCK_N // 2)], x0_t[:]
                                 ).then_inc(s_x0, 16)

            def load_pair0(n0):
                for jj in range(JT):
                    rows = slice(jj * FIELDS, (jj + 1) * FIELDS)
                    tiles = T0 if jj * FIELDS < LAST0 else T0 - 1
                    sp.dma_start(pair0[rows, 0:tiles, :],
                                 bass.AP(x0_rows, n0 + jj * N, [[N, FIELDS], [JT * N, tiles], [1, CH]])
                                 ).then_inc(s_pair0, 16)
                    sp.dma_start(pair0[rows, T0, :],
                                 bass.AP(x0_rows, n0, [[N, FIELDS], [1, CH]])).then_inc(s_pair0, 16)

            def load_xh(dst, tile, n0, done):
                for odd in range(2):
                    tiles = min(dst.shape[1], (FIELDS - odd + 1) // 2 - tile)
                    sp.dma_start(dst[odd * HALF:(odd + 1) * HALF, 0:tiles, :],
                                 bass.AP(x0_rows, n0 + (2 * tile + odd) * N, [[0, HALF], [2 * N, tiles], [1, CH]])
                                 ).then_inc(done, 16)

            def load_back(g, n0):
                load_xh(xh_back[:, g * GT:(g + 1) * GT, :], (FRONT + g) * GT, n0, s_back[g])

            store_x0(0, 0)
            sp.wait_ge(s_x0, 32)
            sp.wait_ge(s_zeroed, ZEROED)
            load_pair0(0)
            load_xh(xh_front[:, 0], 0, 0, s_front[0])
            for g in range(BACK):
                load_back(g, 0)
            store_x0(0, 1)

            def step(t, c):
                n0 = t * BLOCK_N + (c + 1) * CH
                if c == 1:
                    sp.wait_ge(s_x0, t * 64 + 64)
                if c == CPB - 1:
                    sp.wait_ge(s_x0, t * 64 + 96)
                sp.wait_ge(s_prod, number(t, c, 0))
                load_pair0(n0)
                load_xh(xh_front[:, (c + 1) % 2], 0, n0, s_front[(c + 1) % 2])
                for g in range(BACK):
                    sp.wait_ge(s_prod, number(t, c, K2 + FRONT + g + 1))
                    load_back(g, n0)
                if c >= 2 and not isinstance(t, int):
                    store_x0(t + 1, c - 2)

            with sp.Fori(0, BLOCKS - 1) as t:
                for c in range(CPB):
                    step(t, c)
            for c in range(CPB - 1):
                step(BLOCKS - 1, c)
            sp.dma_start(wt1_sb, wt1[0:2 * P, :].rearrange("(k p) m -> p k m", p=P)).then_inc(s_top, 16)
            sp.dma_start(wt1d_sb, wt1[2 * P:2 * P + D, :]).then_inc(s_top, 16)
            sp.dma_start(wt2_sb, wt2.rearrange("(k p) m -> p k m", p=P)).then_inc(s_top, 16)
            sp.dma_start(dense_sb, dense.rearrange("(t p) c -> p t c", p=P)).then_inc(s_top, 16)
            sp.wait_ge(s_ya, B // CH)
            sp.dma_start(out.rearrange("b o -> o b"), y_sb).then_inc(s_out, 16)
            sp.wait_ge(s_out, 16)

        @block.gpsimd
        def _(pool):
            def copy_ids(t):
                pool.tensor_copy(ids_cur[:], ids_sb[:, bass.ds(t, 1), :]).then_inc(s_idcur, 1)
                pool.wait_ge(s_idcur, t + 1)
                pool.sem_inc(s_blocks, 1)

            def gather(fields):
                for f in fields:
                    pool.indirect_dma_start(emb[:, f, :], None, tables[f],
                                            bass.IndirectOffsetOnAxis(ap=ids_cur[:, f:f + 1], axis=0)
                                            ).then_inc(s_gather, 16)

            pool.wait_ge(s_ids, 16)
            copy_ids(0)
            gather(range(FIELDS))
            count_phantoms(pool, s_low["pool"], BY["pool"], AHEAD)
            count_phantoms(pool, s_low["pool"], BY["pool"], BEHIND)
            pool.wait_ge(s_gather, 16 * FIELDS)
            pool.wait_ge(s_turn, CPB)
            copy_ids(1)
            gather(range(THIRD))

            def step(t, c):
                lows = [k for k in BY["pool"] if not is_last(t, c) or k not in ZERO]
                todo = []
                if c < 2 and not (isinstance(t, int) and t == BLOCKS - 1):
                    todo = list(range((c + 1) * THIRD, (c + 2) * THIRD))
                if c == CPB - 1 and not isinstance(t, int):
                    todo = list(range(THIRD))
                for n, k in enumerate(lows):
                    make_low(pool, "pool", t, c, k)
                    if n == 0 and c == CPB - 1 and todo:
                        pool.wait_ge(s_gather, t * (16 * FIELDS) + 2 * 16 * FIELDS)
                        pool.wait_ge(s_turn, t * CPB + 2 * CPB)
                        copy_ids(t + 2)
                    gather(todo[sum(LOOKUPS[:n]):sum(LOOKUPS[:n + 1])])
                    if is_last(t, c) and k == max(x for x in BY["pool"] if x < K0):
                        count_phantoms(pool, s_low["pool"], BY["pool"], ZERO, *LAST)

            with pool.Fori(0, BLOCKS - 2) as t:
                for c in range(CPB):
                    step(t, c)
            for t in (BLOCKS - 2, BLOCKS - 1):
                for c in range(CPB):
                    step(t, c)

        @block.scalar
        def _(act):
            act.wait_ge(s_zeroed, 1)
            for k in [*AHEAD, *BEHIND]:
                layer, tiles = group_tiles(k)
                w = (w1, w2)[layer - 1].rearrange("h k s -> (h k) s")
                whole = [n for n in tiles if n < TK - 1]
                act.dma_start(weight(layer, tiles[0], len(whole)),
                              w[tiles[0] * P:(whole[-1] + 1) * P, :].rearrange("(t p) s -> p t s", p=P)
                              ).then_inc(s_w, 16)
                if tiles[-1] == TK - 1:
                    act.dma_start(weight(layer, TK - 1)[0:HALF, :], w[(TK - 1) * P:, :]).then_inc(s_w, 16)
            act.wait_ge(s_w, 16 * W_DMAS)
            act.activation(w_high[:], w_stage, ACT.Copy).then_inc(s_whigh, 1)
            for j in range(1, SHIFTS):
                tile, p0 = j // JT, (j % JT) * FIELDS
                for wrap, lo, hi in ((0, 0, FIELDS - j), (1, FIELDS - j, FIELDS)):
                    k0 = lo + j - wrap * FIELDS
                    act.dma_start(w0_swapped[p0 + lo:p0 + hi, tile, :],
                                  bass.AP(w0.tensor, (k0 * FIELDS + lo) * S, [[(FIELDS + 1) * S, hi - lo], [1, S]])
                                  ).then_inc(s_w0, 16)
            for n, b in enumerate((b0, b1, b2)):
                act.dma_start(bias_sb[:, n:n + 1], b.rearrange("(s o) -> s o", o=1)).then_inc(s_small, 16)
            act.dma_start(bt1_sb[:], bt1.rearrange("(m p) -> p m", p=P), allow_slow_non_contiguous=True
                          ).then_inc(s_small, 16)
            act.dma_start(bt2_sb[:], bt2.rearrange("(m p) -> p m", p=P), allow_slow_non_contiguous=True
                          ).then_inc(s_small, 16)
            act.dma_start(wt3_sb[:], wt3.rearrange("(k p) o -> p k o", p=P), allow_slow_non_contiguous=True
                          ).then_inc(s_small, 16)
            act.sem_inc(s_act[1], 1)

            def evacuate_turn(t, r):
                act.wait_ge(s_turn, t * CPB + (r + 1))
                act.activation(x0_t[:, (r % 2) * CH:(r % 2 + 1) * CH], turn[r % 2][0:FIELDS, :], ACT.Copy).then_inc(s_turned, 1)

            def relu(dst, layer, lo, hi):
                return act.activation(dst, z[layer][lo:hi, :], ACT.Relu, bias=bias_sb[lo:hi, layer:layer + 1])

            def activate0(parity):
                relu(xk[1][0:HALF, :], 0, 0, HALF)
                relu(xk[1][HALF:S, :], 0, 0, HALF).then_inc(s_xk[1], 1)
                relu(direct01[0:HALF, parity, :], 0, HALF, S).then_inc(s_act[0], 1)

            def make_highs(t, c, ks):
                for k in ks:
                    if k not in SPLIT:
                        continue
                    layer, tiles = group_tiles(k)
                    rows = ROWS0 if layer == 0 else P
                    wait_slot(act, t, c, k, HIGHS)
                    act.wait_ge(s_prod, number(t, c, k + 1))
                    act.activation(high[0:rows, slot(c, k, HIGHS), 0:len(tiles), :], prod[0:rows, k % RING, 0:len(tiles), :],
                                   ACT.Copy).then_inc(s_high, 1)

            for r in range(CPB):
                if r == 2:
                    act.wait_ge(s_x0, 32)
                evacuate_turn(0, r)
            act.wait_ge(s_zeroed, ZEROED)
            act.wait_ge(s_small, 6 * 16)
            count_phantoms(act, s_high, SPLIT_ORDER, AHEAD)
            make_highs(0, -1, ZERO)
            count_phantoms(act, s_high, SPLIT_ORDER, BEHIND)
            act.wait_ge(s_summed, number(0, -1, K2))
            activate0(0)

            def step(t, c):
                last = is_last(t, c)
                make_highs(t, c, AHEAD)
                act.wait_ge(s_summed, number(t, c, 0))
                if c % 2:
                    act.wait_ge(s_red2, t * 2 + (c + 1) // 2)
                relu(direct2[:, (c + 1) % 2, :], 2, 0, S).then_inc(s_act[2], 1)
                if not last:
                    make_highs(t, c, ZERO)
                act.wait_ge(s_summed, number(t, c, K0))
                act.wait_ge(s_prod, number(t, c, 0))
                relu(xk[2][0:HALF, :], 1, 0, HALF)
                relu(xk[2][HALF:S, :], 1, 0, HALF).then_inc(s_xk[2], 1)
                relu(direct01[HALF:S, c % 2, :], 1, HALF, S).then_inc(s_act[1], 1)
                if c >= 2 and not isinstance(t, int):
                    act.wait_ge(s_x0, t * 64 + (64 + (c - 2) * 32))
                    evacuate_turn(t + 1, 2 * (c - 2))
                    evacuate_turn(t + 1, 2 * (c - 2) + 1)
                if not last:
                    act.wait_ge(s_summed, number(t, c, K2))
                    act.wait_ge(s_prod, number(t, c, K0))
                    if c % 2:
                        act.wait_ge(s_red01, t * 2 + (c + 1) // 2)
                    activate0((c + 1) % 2)
                else:
                    count_phantoms(act, s_high, SPLIT_ORDER, ZERO, *LAST)
                make_highs(t, c, BEHIND)

            with act.Fori(0, BLOCKS - 1) as t:
                for c in range(CPB):
                    step(t, c)
            for c in range(CPB):
                step(BLOCKS - 1, c)
            act.wait_ge(s_summed, number(*LAST, PER))
            act.wait_ge(s_red2, 2 * BLOCKS)
            relu(direct2[:, 1, :], 2, 0, S).then_inc(s_act[2], 1)

            for r in range(B // CH):
                act.wait_ge(s_dt, r + 1)
                act.activation(dense_t[:, r, :], turn[r % 2][0:D, :], ACT.Copy).then_inc(s_dte, 1)
            for q in range(B // CH):
                for m in range(M1):
                    act.wait_ge(s_h1, q * M1 + m + 1)
                    if q:
                        act.wait_ge(s_h2, q * M2)
                    act.activation(h1[:, m, :], z[m % 2][:], ACT.Relu, bias=bt1_sb[:, m:m + 1]).then_inc(s_h1a, 1)
                for m in range(M2):
                    act.wait_ge(s_h2, q * M2 + m + 1)
                    if q:
                        act.wait_ge(s_y, q)
                    act.activation(h2[:, m, :], xk[1 + m][:], ACT.Relu, bias=bt2_sb[:, m:m + 1]).then_inc(s_h2a, 1)
                act.wait_ge(s_y, q + 1)
                act.activation(y_sb[:, q * CH:(q + 1) * CH], z[2][0:1, :], ACT.Copy).then_inc(s_ya, 1)

        @block.vector
        def _(dve):
            dve.memset(stage, 0.0).then_inc(s_zeroed, 1)
            dve.memset(pair0[0:ROWS0, T0 - 1, :], 0.0).then_inc(s_zeroed, 1)
            dve.memset(xh_back[HALF:S, BACK * GT - 1, :], 0.0).then_inc(s_zeroed, 1)
            dve.memset(direct2[:], 0.0).then_inc(s_zeroed, 1)
            dve.memset(z[2][:], 0.0).then_inc(s_zeroed, 1)
            dve.memset(part2[:], 0.0).then_inc(s_zeroed, 1)
            dve.wait_ge(s_whigh, 1)
            dve.tensor_tensor(w_low[:], w_stage, w_high[:].bitcast(F32), ALU.subtract).then_inc(s_wlow, 1)
            dve.wait_ge(s_w0, 16 * (4 * (SHIFTS - 1) + 1))
            for rows, tile, many in ((ROWS0, 0, T0 - 1), (LAST0, T0 - 1, 1)):
                w = weight(0, tile, many)[0:rows]
                ins = dve.tensor_tensor(w, w, w0_swapped[0:rows, tile:tile + many, :], ALU.add)
            ins.then_inc(s_w0sum, 1)
            dve.wait_ge(s_wlow, 1)
            dve.wait_ge(s_w0sum, 1)

            def multiply(t, c, k, first):
                layer, tiles = group_tiles(k)
                many = len(tiles)
                if layer == 0:
                    rows, one, other = ROWS0, pair0[0:ROWS0, tiles[0]:tiles[0] + many, :], pair0[0:ROWS0, T0, :]
                else:
                    rows, other = P, xk[layer][:]
                    if tiles[0] < FRONT * GT:
                        one = xh_front[:, c % 2, tiles[0]:tiles[0] + many, :]
                    else:
                        at = tiles[0] - FRONT * GT
                        one = xh_back[:, at:at + many, :]
                        if layer == 1:
                            dve.wait_ge(s_back[at // GT], t * (32 * CPB) + (c + 1) * 32)
                if not first:
                    before = k - RING
                    kind = SPLIT.get(before % PER)
                    if kind:
                        dve.wait_ge(s_low[kind], made(t, c + before // PER, before % PER, BY[kind]))
                    else:
                        dve.wait_ge(s_summed, number(t, c, before + 1))
                dve.tensor_tensor(prod[0:rows, k % RING, 0:many, :], one,
                                  other.unsqueeze(1).broadcast_to([rows, many, CH]), ALU.mult).then_inc(s_prod, 1)

            pending = []

            def products(t, c, ks, first=False):
                for k in ks:
                    multiply(t, c, k, first)
                    flush()
                    if k in BY["dve"]:
                        pending.append((t, c, k))

            def flush():
                while pending:
                    make_low(dve, "dve", *pending.pop())

            def reduce(dst, src, done):
                dve.tensor_reduce(dst, src[:].rearrange("p s (d b) -> p b (s d)", b=P), AX_X, ALU.add).then_inc(done, 1)

            def layer1(t, c):
                dve.wait_ge(s_xk[1], t * CPB + (c + 1))
                dve.wait_ge(s_front[c % 2], t * (32 * CPB // 2) + (c // 2 + 1) * 32)
                products(t, c, AHEAD)

            count_phantoms(dve, s_prod, ALL, AHEAD)
            count_phantoms(dve, s_low["dve"], BY["dve"], AHEAD)
            dve.wait_ge(s_pair0, 16 * 2 * JT)
            products(0, -1, ZERO, first=True)
            flush()
            count_phantoms(dve, s_prod, ALL, BEHIND)
            count_phantoms(dve, s_low["dve"], BY["dve"], BEHIND)
            layer1(0, 0)
            flush()

            def step(t, c):
                chunk = t * CPB + c
                last = is_last(t, c)
                if last:
                    count_phantoms(dve, s_prod, ALL, ZERO, *LAST)
                    count_phantoms(dve, s_low["dve"], BY["dve"], ZERO, *LAST)
                else:
                    dve.wait_ge(s_pair0, chunk * (16 * 2 * JT) + 2 * 16 * 2 * JT)
                    products(t, c, ZERO)
                    flush()
                if c == 0:
                    dve.wait_ge(s_act[2], chunk + 1)
                    reduce(part2[:, 1, :], direct2, s_red2)
                    dve.wait_ge(s_red2, t * 2 + 1)
                    dve.tensor_tensor(sum2[:, bass.ds(t, 1), :], part2[:, 0:1, :], part2[:, 1:2, :],
                                      ALU.add).then_inc(s_sum2, 1)
                if c == 2:
                    dve.wait_ge(s_act[2], chunk + 1)
                    reduce(part2[:, 0, :], direct2, s_red2)
                dve.wait_ge(s_xk[2], chunk + 1)
                products(t, c, BEHIND[:1])
                if c % 2:
                    dve.wait_ge(s_act[1], chunk + 2)
                    reduce(part01[:, c // 2, :], direct01, s_red01)
                products(t, c, BEHIND[1:])
                if not last:
                    layer1(t, c + 1)
                flush()
                if c == CPB - 1:
                    dve.wait_ge(s_red01, t * 2 + 2)
                    dve.tensor_tensor(sum01[:, bass.ds(t, 1), :], part01[:, 0:1, :], part01[:, 1:2, :],
                                      ALU.add).then_inc(s_sum01, 1)

            with dve.Fori(0, BLOCKS - 1) as t:
                for c in range(CPB):
                    step(t, c)
            for c in range(CPB):
                step(BLOCKS - 1, c)
            dve.wait_ge(s_act[2], CHUNKS + 1)
            reduce(part2[:, 1, :], direct2, s_red2)
            dve.wait_ge(s_red2, 2 * BLOCKS + 1)
            dve.tensor_tensor(sum2[:, BLOCKS, :], part2[:, 0, :], part2[:, 1, :], ALU.add).then_inc(s_sum2, 1)

        @block.tensor
        def _(pe):
            def turn_round(r):
                for q in range(DC):
                    mm = pe.transpose(turn[r % 2][0:FIELDS, q * P:(q + 1) * P], emb[:, :, r * DC + q], eye_sb[:])
                mm.then_inc(s_turn, 1)

            def sum_groups(t, c, ks):
                for k in ks:
                    layer, tiles = group_tiles(k)
                    first, last = k == ks[0], k == ks[-1]
                    jobs = [(n, tile, tile_rows(layer, tile)) for n, tile in enumerate(tiles)]
                    if k not in SPLIT:
                        pe.wait_ge(s_prod, number(t, c, k + 1))
                        for n, tile, rows in jobs:
                            mm = pe.matmul(z[layer][:], weight(layer, tile)[0:rows, :], prod[0:rows, k % RING, n, :],
                                           start=first and n == 0, stop=last and n == len(tiles) - 1)
                        mm.then_inc(s_summed, 1)
                        continue
                    pe.wait_ge(s_high, made(t, c, k, SPLIT_ORDER))
                    for w in (w_high, w_low):
                        for n, tile, rows in jobs:
                            pe.matmul(z[layer][:], w[0:rows, SPLIT_TILES.index((layer, tile)), :],
                                      high[0:rows, slot(c, k, HIGHS), n, :], start=first and n == 0 and w is w_high, stop=False)
                    pe.wait_ge(s_low[SPLIT[k]], made(t, c, k, BY[SPLIT[k]]))
                    for n, tile, rows in jobs:
                        mm = pe.matmul(z[layer][:], w_high[0:rows, SPLIT_TILES.index((layer, tile)), :],
                                       low[0:rows, slot(c, k, LOWS), n, :], start=False, stop=last and n == len(tiles) - 1)
                    mm.then_inc(s_summed, 1)

            pe.wait_ge(s_eye, 16)
            pe.wait_ge(s_gather, 16 * FIELDS)
            for r in range(CPB):
                if r >= 2:
                    pe.wait_ge(s_turned, r - 1)
                turn_round(r)
            pe.wait_ge(s_wlow, 1)
            pe.wait_ge(s_w0sum, 1)
            count_phantoms(pe, s_summed, ALL, AHEAD)
            sum_groups(0, -1, ZERO)
            count_phantoms(pe, s_summed, ALL, BEHIND)

            def step(t, c):
                chunk = t * CPB + c
                last = is_last(t, c)
                turns = c == 2 and not isinstance(t, int)
                if turns:
                    pe.wait_ge(s_gather, t * (16 * FIELDS) + 2 * 16 * FIELDS)
                    pe.wait_ge(s_turned, t * CPB + CPB)
                pe.wait_ge(s_act[1], chunk + 1)
                sum_groups(t, c, AHEAD)
                if turns:
                    turn_round(0)
                    turn_round(1)
                if last:
                    count_phantoms(pe, s_summed, ALL, ZERO, *LAST)
                else:
                    pe.wait_ge(s_act[0], chunk + 1)
                    sum_groups(t, c, ZERO)
                if turns:
                    pe.wait_ge(s_turned, t * CPB + (CPB + 2))
                pe.wait_ge(s_act[2], chunk + 1)
                sum_groups(t, c, BEHIND)
                if turns:
                    turn_round(2)
                    turn_round(3)

            with pe.Fori(0, BLOCKS - 1) as t:
                for c in range(CPB):
                    step(t, c)
            for c in range(CPB):
                step(BLOCKS - 1, c)

            pe.wait_ge(s_small, 6 * 16)
            pe.wait_ge(s_top, 4 * 16)
            for r in range(B // CH):
                if r >= 2:
                    pe.wait_ge(s_dte, r - 1)
                for q in range(DC):
                    mm = pe.transpose(turn[r % 2][0:D, q * P:(q + 1) * P], dense_sb[:, r * DC + q, :], eye_sb[:])
                mm.then_inc(s_dt, 1)
            pe.wait_ge(s_sum01, BLOCKS)
            pe.wait_ge(s_sum2, BLOCKS + 1)
            pe.wait_ge(s_act[2], CHUNKS + 1)
            for q in range(B // CH):
                blocks = slice(q * DC, (q + 1) * DC)
                cin2 = slice(q * DC + 1, (q + 1) * DC + 1)
                pe.wait_ge(s_dte, q + 1)
                for m in range(M1):
                    if q * M1 + m >= 2:
                        pe.wait_ge(s_h1a, q * M1 + m - 1)
                    cols = slice(m * P, (m + 1) * P)
                    pe.matmul(z[m % 2][:], wt1_sb[:, 0, cols],
                              sum01[:, blocks, :].rearrange("p t b -> p (t b)"), start=True, stop=False)
                    pe.matmul(z[m % 2][:], wt1_sb[:, 1, cols],
                              sum2[:, cin2, :].rearrange("p t b -> p (t b)"), start=False, stop=False)
                    pe.matmul(z[m % 2][:], wt1d_sb[:, cols], dense_t[:, q, :],
                              start=False, stop=True).then_inc(s_h1, 1)
                for m in range(M2):
                    if q:
                        pe.wait_ge(s_h2a, q * M2 - M2 + m + 1)
                    for k in range(M1):
                        pe.wait_ge(s_h1a, q * M1 + k + 1)
                        mm = pe.matmul(xk[1 + m][:], wt2_sb[:, k, m * P:(m + 1) * P], h1[:, k, :],
                                       start=k == 0, stop=k == M1 - 1)
                    mm.then_inc(s_h2, 1)
                if q:
                    pe.wait_ge(s_ya, q)
                pe.wait_ge(s_h2a, (q + 1) * M2)
                for k in range(M2):
                    mm = pe.matmul(z[2][0:1, :], wt3_sb[:, k, :], h2[:, k, :], start=k == 0, stop=k == M2 - 1)
                mm.then_inc(s_y, 1)


_TABLES = [f"tbl_{f}" for f in range(FIELDS)]
_INS = ["dense_ctx", "ids", *_TABLES, "L0_rec_w0", "L0_rec_w1", "L0_rec_w2", "L0_rec_b0", "L0_rec_b1",
        "L0_rec_b2", "W_top1", "b_top1", "W_top2", "b_top2", "W_top3"]


def kernel(**inputs):
    import numpy as np
    import concourse.bacc as bacc
    from concourse.bass_utils import run_bass_kernel_spmd

    nc = bacc.Bacc("TRN2", target_bir_lowering=False, num_devices=1)
    arrays, aps = {}, {}
    for name in _INS:
        a = np.ascontiguousarray(inputs[name])
        arrays[f"in_{name}_dram"] = a
        aps[name] = nc.dram_tensor(f"in_{name}_dram", a.shape, mybir.dt.from_np(a.dtype), kind="ExternalInput").ap()
    arrays["in_eye_dram"] = np.eye(P, dtype=np.float32)
    eye = nc.dram_tensor("in_eye_dram", (P, P), F32, kind="ExternalInput").ap()
    out = nc.dram_tensor("out_0_dram", (inputs["ids"].shape[0], 1), F32, kind="ExternalOutput").ap()
    rest = [aps[name] for name in _INS[2 + FIELDS:]]
    build(nc, aps["dense_ctx"], aps["ids"], [aps[name] for name in _TABLES], *rest, eye, out)
    r = run_bass_kernel_spmd(nc, [arrays], core_ids=[0])
    return r.results[0]["out_0_dram"]
```
